# Optimizing a Trainium2 kernel written in Bass

```python
import numpy as np
import jax
import jax.numpy as jnp

def _softmax(x, axis=-1):
    return jax.nn.softmax(x, axis=axis)

def _gelu(x):
    return jax.nn.gelu(x, approximate=True)

def _silu(x):
    return jax.nn.silu(x)

def _sigmoid(x):
    return jax.nn.sigmoid(x)

def _layernorm(x, axis=-1, eps=1e-05):
    m = jnp.mean(x, axis=axis, keepdims=True)
    v = jnp.var(x, axis=axis, keepdims=True)
    return (x - m) / jnp.sqrt(v + eps)

def _scatter_add(tgt, idx, src, axis=0):
    return tgt.at[idx].add(src)

def _segment_sum(src, seg, n):
    return jax.ops.segment_sum(src, seg, n)
kernel_name = 'mk_prb_d1_jaxref_r8_9d3cb8'

def setup_inputs(seed: int=0):
    np.random.seed(seed)
    _w = jnp.asarray

    def _L0_attn_setup():
        import jax, jax.numpy as jnp
        import numpy as np
        B, T, D, L, K = (4, 256, 256, 256, 4)

        def _reference_tuple_inner(x, w_y, b_y, w_x, b_x, conv_w, conv_b, a_param, w_ig, b_ig, w_ag, b_ag, w_out, b_out):
            Tn = x.shape[1]
            y = jax.nn.gelu(jnp.einsum('btd,dl->btl', x, w_y) + b_y, approximate=False)
            xb = jnp.einsum('btd,dl->btl', x, w_x) + b_x
            xp = jnp.pad(xb, ((0, 0), (K - 1, 0), (0, 0)))
            conv = conv_b
            for k in range(K):
                conv = conv + conv_w[k] * xp[:, k:k + Tn]
            gate_x = jax.nn.sigmoid(jnp.einsum('btl,lm->btm', conv, w_ig) + b_ig)
            gate_a = jax.nn.sigmoid(jnp.einsum('btl,lm->btm', conv, w_ag) + b_ag)
            log_a = -8.0 * gate_a * jax.nn.softplus(a_param)
            a = jnp.exp(log_a)
            mult = jnp.sqrt(1.0 - jnp.exp(2.0 * log_a))
            reset = (jnp.arange(Tn) == 0)[None, :, None]
            a = jnp.where(reset, 0.0, a)
            mult = jnp.where(reset, 1.0, mult)
            nx = gate_x * conv * mult

            def step(h, inp):
                a_t, x_t = inp
                h = a_t * h + x_t
                return (h, h)
            h0 = jnp.zeros((x.shape[0], a.shape[-1]), x.dtype)
            hn, hs = jax.lax.scan(step, h0, (a.transpose(1, 0, 2), nx.transpose(1, 0, 2)))
            h_seq = hs.transpose(1, 0, 2)
            out = jnp.einsum('btl,ld->btd', h_seq * y, w_out) + b_out
            return (out, hn)
        key = jax.random.key(seed)
        ks = jax.random.split(key, 12)
        s = 0.02
        f32 = jnp.float32
        return {'x': jax.random.normal(ks[0], (B, T, D), f32), 'w_y': jax.random.normal(ks[1], (D, L), f32) * s, 'b_y': jnp.zeros((L,), f32), 'w_x': jax.random.normal(ks[2], (D, L), f32) * s, 'b_x': jnp.zeros((L,), f32), 'conv_w': jax.random.normal(ks[3], (K, L), f32) * s, 'conv_b': jnp.zeros((L,), f32), 'a_param': jax.random.uniform(ks[4], (L,), f32, 0.5, 4.0), 'w_ig': jax.random.normal(ks[5], (L, L), f32) * s, 'b_ig': jnp.zeros((L,), f32), 'w_ag': jax.random.normal(ks[6], (L, L), f32) * s, 'b_ag': jnp.zeros((L,), f32), 'w_out': jax.random.normal(ks[7], (L, D), f32) * s, 'b_out': jnp.zeros((D,), f32)}
    _L0_attn_in = _L0_attn_setup()

    def _L0_ffn_setup():
        import jax, jax.numpy as jnp
        import numpy as np
        D_MODEL = 256
        HIDDEN = int(2 * D_MODEL * 4 / 3)

        def ternary_quant(w):
            s = jnp.mean(jnp.abs(w))
            q = jnp.clip(jnp.round(w / s), -1.0, 1.0) * s
            return w + jax.lax.stop_gradient(q - w)
        key = jax.random.key(seed)
        k0, k1, k2, k3 = jax.random.split(key, 4)
        x = jax.random.normal(k0, (4, 512, D_MODEL), dtype=jnp.float32)
        std_in = 1.0 / np.sqrt(D_MODEL)
        std_h = 1.0 / np.sqrt(HIDDEN)
        w1 = jax.random.uniform(k1, (HIDDEN, D_MODEL), jnp.float32, -std_in, std_in)
        w3 = jax.random.uniform(k2, (HIDDEN, D_MODEL), jnp.float32, -std_in, std_in)
        w2 = jax.random.uniform(k3, (D_MODEL, HIDDEN), jnp.float32, -std_h, std_h)
        return {'x': x, 'w1': w1, 'w3': w3, 'w2': w2}
    _L0_ffn_in = _L0_ffn_setup()
    _d = {'L0_attn_x': _L0_attn_in['x'], 'L0_attn_w_y': _L0_attn_in['w_y'], 'L0_attn_b_y': _L0_attn_in['b_y'], 'L0_attn_w_x': _L0_attn_in['w_x'], 'L0_attn_b_x': _L0_attn_in['b_x'], 'L0_attn_conv_w': _L0_attn_in['conv_w'], 'L0_attn_conv_b': _L0_attn_in['conv_b'], 'L0_attn_a_param': _L0_attn_in['a_param'], 'L0_attn_w_ig': _L0_attn_in['w_ig'], 'L0_attn_b_ig': _L0_attn_in['b_ig'], 'L0_attn_w_ag': _L0_attn_in['w_ag'], 'L0_attn_b_ag': _L0_attn_in['b_ag'], 'L0_attn_w_out': _L0_attn_in['w_out'], 'L0_attn_b_out': _L0_attn_in['b_out'], 'L0_ffn_w1': _L0_ffn_in['w1'], 'L0_ffn_w3': _L0_ffn_in['w3'], 'L0_ffn_w2': _L0_ffn_in['w2']}
    _x0 = _d['L0_attn_x']
    _d['L0_attn_x'] = jax.random.normal(jax.random.fold_in(jax.random.key(seed), 1), (2, 512, 256), dtype=_x0.dtype)
    del _x0
    return _d

def reference(L0_attn_x, L0_attn_w_y, L0_attn_b_y, L0_attn_w_x, L0_attn_b_x, L0_attn_conv_w, L0_attn_conv_b, L0_attn_a_param, L0_attn_w_ig, L0_attn_b_ig, L0_attn_w_ag, L0_attn_b_ag, L0_attn_w_out, L0_attn_b_out, L0_ffn_w1, L0_ffn_w3, L0_ffn_w2):

    def _L0_attn_ref(x, w_y, b_y, w_x, b_x, conv_w, conv_b, a_param, w_ig, b_ig, w_ag, b_ag, w_out, b_out):
        import jax, jax.numpy as jnp
        import numpy as np
        B, T, D, L, K = (4, 256, 256, 256, 4)

        def _reference_tuple_inner(x, w_y, b_y, w_x, b_x, conv_w, conv_b, a_param, w_ig, b_ig, w_ag, b_ag, w_out, b_out):
            Tn = x.shape[1]
            y = jax.nn.gelu(jnp.einsum('btd,dl->btl', x, w_y) + b_y, approximate=False)
            xb = jnp.einsum('btd,dl->btl', x, w_x) + b_x
            xp = jnp.pad(xb, ((0, 0), (K - 1, 0), (0, 0)))
            conv = conv_b
            for k in range(K):
                conv = conv + conv_w[k] * xp[:, k:k + Tn]
            gate_x = jax.nn.sigmoid(jnp.einsum('btl,lm->btm', conv, w_ig) + b_ig)
            gate_a = jax.nn.sigmoid(jnp.einsum('btl,lm->btm', conv, w_ag) + b_ag)
            log_a = -8.0 * gate_a * jax.nn.softplus(a_param)
            a = jnp.exp(log_a)
            mult = jnp.sqrt(1.0 - jnp.exp(2.0 * log_a))
            reset = (jnp.arange(Tn) == 0)[None, :, None]
            a = jnp.where(reset, 0.0, a)
            mult = jnp.where(reset, 1.0, mult)
            nx = gate_x * conv * mult

            def step(h, inp):
                a_t, x_t = inp
                h = a_t * h + x_t
                return (h, h)
            h0 = jnp.zeros((x.shape[0], a.shape[-1]), x.dtype)
            hn, hs = jax.lax.scan(step, h0, (a.transpose(1, 0, 2), nx.transpose(1, 0, 2)))
            h_seq = hs.transpose(1, 0, 2)
            out = jnp.einsum('btl,ld->btd', h_seq * y, w_out) + b_out
            return (out, hn)
        return _reference_tuple_inner(x, w_y, b_y, w_x, b_x, conv_w, conv_b, a_param, w_ig, b_ig, w_ag, b_ag, w_out, b_out)[0]

    def _L0_ffn_ref(x, w1, w3, w2):
        import jax, jax.numpy as jnp
        import numpy as np
        D_MODEL = 256
        HIDDEN = int(2 * D_MODEL * 4 / 3)

        def ternary_quant(w):
            s = jnp.mean(jnp.abs(w))
            q = jnp.clip(jnp.round(w / s), -1.0, 1.0) * s
            return w + jax.lax.stop_gradient(q - w)
        w1q = ternary_quant(w1)
        w3q = ternary_quant(w3)
        w2q = ternary_quant(w2)
        h1 = jnp.einsum('bsd,hd->bsh', x, w1q)
        h3 = jnp.einsum('bsd,hd->bsh', x, w3q)
        g = jax.nn.silu(h1) * h3
        return jnp.einsum('bsh,dh->bsd', g, w2q)
    x = L0_attn_x
    xn = _layernorm(x, axis=-1)
    x = x + _L0_attn_ref(xn, L0_attn_w_y, L0_attn_b_y, L0_attn_w_x, L0_attn_b_x, L0_attn_conv_w, L0_attn_conv_b, L0_attn_a_param, L0_attn_w_ig, L0_attn_b_ig, L0_attn_w_ag, L0_attn_b_ag, L0_attn_w_out, L0_attn_b_out) + _L0_ffn_ref(xn, L0_ffn_w1, L0_ffn_w3, L0_ffn_w2)
    return x

_drawn_inputs = setup_inputs


def setup_inputs(seed=0):
    import zlib

    import numpy as np

    out = dict(_drawn_inputs(seed))
    spreads = {'L0_attn_b_y': (0.0, 0.8),
     'L0_attn_b_x': (0.0, 0.8),
     'L0_attn_conv_b': (0.0, 0.8),
     'L0_attn_b_ig': (0.0, 0.8),
     'L0_attn_b_ag': (0.0, 0.8),
     'L0_attn_b_out': (0.0, 0.299)}
    factors = {'L0_attn_w_y': 8.0,
     'L0_attn_w_x': 8.0,
     'L0_attn_conv_w': 8.0,
     'L0_attn_a_param': 8.0,
     'L0_attn_w_ig': 8.0,
     'L0_attn_w_ag': 8.0,
     'L0_attn_w_out': 8.0,
     'L0_ffn_w1': 4.091,
     'L0_ffn_w3': 3.604,
     'L0_ffn_w2': 3.605}
    for name, (base, spread) in spreads.items():
        noise = np.random.default_rng([zlib.crc32(name.encode()), seed]).standard_normal(out[name].shape)
        drawn = base * np.exp(spread * noise) if base else spread * noise
        out[name] = jnp.asarray(drawn.astype(out[name].dtype))
    for name, factor in factors.items():
        out[name] = (out[name] * factor).astype(out[name].dtype)
    return out
```

```python
from contextlib import ExitStack

import concourse.bass as bass
from concourse import mybir

P = 128
SEQS, SEQ = 2, 512
TOKENS = SEQS * SEQ
D = 256
HIDDEN = 682
TAPS = 4
KC = D // P
TILES = SEQ // P
FULL = HIDDEN // P
TAIL = HIDDEN - FULL * P
HALF = 64
W3_AT = FULL * P + HALF
W13 = W3_AT + HIDDEN
EPS = 1e-5
WEIGHTS = D * HIDDEN
MAGIC = 1.5 * 2.0 ** 23

B_Y, B_X, CONV_B, A_PARAM, B_IG, B_AG, CONV_W = (KC * i for i in range(7))
PARAMS = CONV_W + KC * TAPS
WX, WY, WIG, WAG, WOUT = range(5)


def build(nc: bass.Bass, x, dense, w13t, w2t, params, b_out, out):
    f32, f32r, bf16 = mybir.dt.float32, mybir.dt.float32r, mybir.dt.bfloat16
    ALU, ACT = mybir.AluOpType, mybir.ActivationFunctionType

    x_dram = x.rearrange("(s t p) d -> s p t d", s=SEQS, p=P)
    out_dram = out.rearrange("(s t p) d -> s p t d", s=SEQS, p=P)

    ctx = ExitStack()
    with ctx:
        def sb(name, shape, dt=f32):
            return ctx.enter_context(nc.sbuf_tensor(name, shape, dt))

        def sem(name):
            return ctx.enter_context(nc.semaphore(name))

        x_sb = sb("x_sb", [P, SEQS, TILES, D])
        xn_y = sb("xn_y", [P, SEQS * TILES * D])
        xn = xn_y[:, :].rearrange("p (s t d) -> p s t d", s=SEQS, t=TILES)
        y = xn_y[:, :].rearrange("p (s c n) -> p s c n", s=SEQS, c=KC)
        xt_hi = sb("xt_hi", [P, SEQS, KC, SEQ], f32r)
        xt_lo = sb("xt_lo", [P, SEQS, KC, SEQ], f32r)
        w_raw = sb("w_raw", [P, 5, KC, D])
        w_hi = sb("w_hi", [P, 5, KC, D], f32r)
        w_lo = sb("w_lo", [P, 5, KC, D], f32r)
        w13_raw = sb("w13_raw", [P, KC, W13])
        w13_q = sb("w13_q", [P, KC, W13], f32r)
        below = sb("below", [P, KC, W13], bf16)
        w2_raw = sb("w2_raw", [P, FULL + 1, D])
        w2_q = sb("w2_q", [P, FULL + 1, D], f32r)
        xb = sb("xb", [P, SEQS, KC, TAPS - 1 + SEQ])
        conv = sb("conv", [P, SEQS, KC, SEQ])
        conv_hi = sb("conv_hi", [P, SEQS, KC, SEQ], f32r)
        conv_lo = sb("conv_lo", [P, SEQS, KC, SEQ], f32r)
        tx = sb("tx", [P, SEQS, KC, SEQ])
        ta = sb("ta", [P, SEQS, KC, SEQ])
        g_hi = sb("g_hi", [P, FULL, SEQS, SEQ], f32r)
        g_lo = sb("g_lo", [P, FULL, SEQS, SEQ], f32r)
        gt = sb("gt", [P, SEQS, SEQ], f32r)
        gt_hi = sb("gt_hi", [P, SEQS, SEQ], f32r)
        RING = 3
        par = sb("par", [P, PARAMS])
        half_b = sb("half_b", [P, 2 * KC])
        a_rate = sb("a_rate", [P, KC])
        sp_e = sb("sp_e", [P, 3, KC])
        b_out_bc = sb("b_out_bc", [P, D])
        ident = sb("ident", [P, P])
        ones = sb("ones", [P, P])
        stats = sb("stats", [P, SEQS, TILES, 6])
        mv = sb("mv", [P, SEQS, TILES, 2])
        ln = sb("ln", [P, 8, SEQS, TILES])
        V, LOG, R0, SQ, VSQ, RSTD, SHIFT = range(7)
        abs_sum = sb("abs_sum", [P, 4])
        thr = sb("thr", [P, 2, 2])
        scale = sb("scale", [P, 3])
        inv_s2 = sb("inv_s2", [P, 1])
        quarter = sb("quarter", [P, 1])
        s32 = sb("s32", [P, 1])

        w_flat = w_raw[:, :, :, :].rearrange("p m c n -> p (m c n)")
        silu = w_flat[:, 0:RING * SEQ].rearrange("p (r n) -> p r n", r=RING)
        silu_t = w_flat[:, RING * SEQ:RING * SEQ + TOKENS]
        w13_flat = w13_raw[:, :, :].rearrange("p c n -> p (c n)")
        g = w13_flat[:, 0:RING * SEQ].rearrange("p (r n) -> p r n", r=RING)
        g_t = w13_flat[:, RING * SEQ:RING * SEQ + TOKENS]

        slot = [ctx.enter_context(nc.psum_tensor(f"slot{i}", [P, 2, SEQ], f32)) for i in range(4)]
        T_SLOT, X_SLOT, Y_SLOT = (0, 1), (2, 3), (0, 1)
        SUM_SLOT = 2
        H_SLOT = ((2, 3, 0, 3, 0), (1, 2, 3, 1, 2))
        TAIL_SLOT = 1
        GX_SLOT, GA_SLOT = (1, 2), (2, 3)
        O_SLOT = (0, 3)
        sums = slot[SUM_SLOT][:, 0, 0:3]

        x_loaded = [sem(f"x_loaded{s}") for s in range(SEQS)]
        w_loaded = [sem(f"w_loaded{m}") for m in range(5)]
        w1_loaded, w3_loaded = sem("w1_loaded"), sem("w3_loaded")
        w2_loaded = sem("w2_loaded")
        par_loaded, b_out_loaded = sem("par_loaded"), sem("b_out_loaded")
        out_stored = sem("out_stored")
        consts_set, ident_set, pads_set = sem("consts_set"), sem("ident_set"), sem("pads_set")
        quarter_set = sem("quarter_set")
        gaps_set = sem("gaps_set")
        stats_set, mv_set, v_set = sem("stats_set"), sem("mv_set"), sem("v_set")
        log_set, r0_set, rstd_step, norm_set = sem("log_set"), sem("r0_set"), sem("rstd_step"), sem("norm_set")
        xn_set, xt_psum, xt_hi_set, xt_lo_set = sem("xn_set"), sem("xt_psum"), sem("xt_hi_set"), sem("xt_lo_set")
        w_hi_set = sem("w_hi_set")
        w_lo_set = sem("w_lo_set")
        sp_abs, sp_exp, sp_log, sp_relu, rate_set, half_b_set = (
            sem("sp_abs"), sem("sp_exp"), sem("sp_log"), sem("sp_relu"), sem("rate_set"), sem("half_b_set"))
        abs13_set, abs2_set, sum13_psum, sum2_psum = (
            sem("abs13_set"), sem("abs2_set"), sem("sum13_psum"), sem("sum2_psum"))
        thr_set, scale2_set, s2_ready = sem("thr_set"), sem("scale2_set"), sem("s2_ready")
        below_set, w13_q_set, w2_round, w2_q_set = sem("below_set"), sem("w13_q_set"), sem("w2_round"), sem("w2_q_set")
        xb_psum, xb_set = sem("xb_psum"), sem("xb_set")
        tap_set, tap_step, conv_set = sem("tap_set"), sem("tap_step"), sem("conv_set")
        conv_hi_set, conv_lo_set = sem("conv_hi_set"), sem("conv_lo_set")
        y_psum, y_set = sem("y_psum"), sem("y_set")
        gx_psum, ga_psum, tx_set, ta_set = sem("gx_psum"), sem("ga_psum"), sem("tx_set"), sem("ta_set")
        a_set, a2_set, mult_set, mult0_set = sem("a_set"), sem("a2_set"), sem("mult_set"), sem("mult0_set")
        nx_step, nx_set, h_set, hy_set = sem("nx_step"), sem("nx_set"), sem("h_set"), sem("hy_set")
        hy_hi_set, hy_lo_set = sem("hy_hi_set"), sem("hy_lo_set")
        h_psum, silu_set, g_set, g_hi_set, g_lo_set = (
            sem("h_psum"), sem("silu_set"), sem("g_set"), sem("g_hi_set"), sem("g_lo_set"))
        t_psum, silu_t_set, g_t_set, gt_hi_set, gt_lo_set = (
            sem("t_psum"), sem("silu_t_set"), sem("g_t_set"), sem("gt_hi_set"), sem("gt_lo_set"))
        x_res_set, o_psum, o_set = sem("x_res_set"), sem("o_psum"), sem("o_set")

        HJ = [(s, j) for s in range(SEQS) for j in range(FULL)]

        block = ctx.enter_context(nc.Block())

        @block.sync
        def _(sp):
            def square(m):
                sp.dma_start(w_raw[:, m], dense[m].rearrange("(c p) n -> p c n", p=P)).then_inc(w_loaded[m], 16)

            sp.dma_start(x_sb[:, 0], x_dram[0]).then_inc(x_loaded[0], 16)
            square(WX)
            sp.dma_start(x_sb[:, 1], x_dram[1]).then_inc(x_loaded[1], 16)
            w13_dram = w13t.rearrange("(c p) n -> p c n", p=P)
            sp.dma_start(w13_raw[:, :, 0:HIDDEN], w13_dram[:, :, 0:HIDDEN]).then_inc(w1_loaded, 16)
            sp.dma_start(w13_raw[:, :, W3_AT:W13], w13_dram[:, :, HIDDEN:2 * HIDDEN]).then_inc(w3_loaded, 16)
            square(WY)
            sp.dma_start(w2_raw[:, 0:FULL], w2t[0:FULL * P].rearrange("(j p) n -> p j n", p=P)).then_inc(w2_loaded, 16)
            sp.wait_ge(gaps_set, 2)
            sp.dma_start(w2_raw[0:TAIL, FULL], w2t[FULL * P:HIDDEN]).then_inc(w2_loaded, 16)
            sp.dma_start(w2_raw[HALF:HALF + TAIL, FULL], w2t[FULL * P:HIDDEN]).then_inc(w2_loaded, 16)
            square(WIG)
            square(WAG)
            square(WOUT)
            for s in range(SEQS):
                for i in range(2):
                    sp.wait_ge(o_set, 2 * s + i + 1)
                    t = slice(i * TILES // 2, (i + 1) * TILES // 2)
                    sp.dma_start(out_dram[s][:, t], x_sb[:, s, t]).then_inc(out_stored, 16)
            sp.wait_ge(out_stored, 16 * 2 * SEQS)

        @block.gpsimd
        def _(pool):
            nc.gpsimd.memset(ident[:, :], 0.0).then_inc(consts_set, 1)
            nc.gpsimd.memset(w13_raw[:, :, HIDDEN:W3_AT], 0.0).then_inc(gaps_set, 1)
            nc.gpsimd.memset(w2_raw[:, FULL, :], 0.0).then_inc(gaps_set, 1)
            pool.wait_ge(consts_set, 1)
            nc.gpsimd.affine_select(out=ident[:, :], in_=ident[:, :], compare_op=ALU.not_equal, fill=1.0, base=0,
                                    pattern=[[-1, P]], channel_multiplier=1).then_inc(ident_set, 1)
            nc.gpsimd.memset(ones[:, :], 1.0).then_inc(consts_set, 1)
            nc.gpsimd.memset(abs_sum[:, 3:4], 0.0).then_inc(consts_set, 1)
            nc.gpsimd.memset(xb[:, :, :, 0:TAPS - 1], 0.0).then_inc(pads_set, 1)
            nc.gpsimd.memset(gt[:, :, :].bitcast(f32), 0.0).then_inc(pads_set, 1)

            def square_lo(m):
                pool.wait_ge(w_hi_set, m + 1)
                nc.gpsimd.tensor_tensor(w_lo[:, m], w_raw[:, m], w_hi[:, m].bitcast(f32), ALU.subtract).then_inc(w_lo_set, 1)

            def newest_tap(s):
                for c in range(KC):
                    pool.wait_ge(xb_set, KC * s + c + 1)
                    k = TAPS - 1
                    nc.gpsimd.tensor_scalar(conv[:, s, c], xb[:, s, c, k:k + SEQ],
                                            par[:, CONV_W + KC * k + c:CONV_W + KC * k + c + 1],
                                            par[:, CONV_B + c:CONV_B + c + 1], ALU.mult, ALU.add).then_inc(tap_set, 1)

            def residual(s):
                pool.wait_ge(xn_set, TILES * (s + 1))
                pool.wait_ge(b_out_loaded, 16)
                for t in range(TILES):
                    nc.gpsimd.tensor_tensor(x_sb[:, s, t], x_sb[:, s, t], b_out_bc[:, :], ALU.add).then_inc(x_res_set, 1)

            def lo_of_conv(s):
                pool.wait_ge(conv_hi_set, s + 1)
                nc.gpsimd.tensor_tensor(conv_lo[:, s], conv[:, s], conv_hi[:, s].bitcast(f32), ALU.subtract).then_inc(conv_lo_set, 1)

            def lo_of_g(n):
                s, j = HJ[n]
                pool.wait_ge(g_hi_set, n + 1)
                nc.gpsimd.tensor_tensor(g_lo[:, j, s], g[:, n % RING], g_hi[:, j, s].bitcast(f32), ALU.subtract).then_inc(g_lo_set, 1)

            square_lo(WX)
            square_lo(WY)
            pool.wait_ge(par_loaded, 16)
            newest_tap(0)
            newest_tap(1)
            square_lo(WIG)
            square_lo(WAG)
            square_lo(WOUT)
            pool.wait_ge(scale2_set, 2)
            nc.gpsimd.tensor_scalar(w2_raw[:, :, :], w2_raw[:, :, :], inv_s2[:, 0:1], MAGIC, ALU.mult, ALU.add).then_inc(w2_round, 1)
            pool.wait_ge(w2_round, 1)
            nc.gpsimd.tensor_scalar(w2_raw[:, :, :], w2_raw[:, :, :], MAGIC + 1.0, MAGIC - 1.0, ALU.min, ALU.max).then_inc(w2_round, 1)
            pool.wait_ge(w2_round, 2)
            nc.gpsimd.tensor_scalar(w2_q[:, :, :], w2_raw[:, :, :], 1.0, -MAGIC, ALU.mult, ALU.add).then_inc(w2_q_set, 1)
            lo_of_conv(0)
            lo_of_g(0)
            lo_of_g(1)
            lo_of_g(2)
            lo_of_conv(1)
            lo_of_g(3)
            lo_of_g(4)
            residual(0)
            residual(1)
            for n in range(FULL, 2 * FULL):
                lo_of_g(n)

        @block.scalar
        def _(act):
            act.dma_start(par[:, :], params).then_inc(par_loaded, 16)
            act.dma_start(b_out_bc[:, :], b_out.partition_broadcast(P)).then_inc(b_out_loaded, 16)

            def square_hi(m):
                act.wait_ge(w_loaded[m], 16)
                nc.scalar.activation(w_hi[:, m], w_raw[:, m], ACT.Copy).then_inc(w_hi_set, 1)

            act.wait_ge(par_loaded, 16)
            a_par = par[:, A_PARAM:A_PARAM + KC]
            nc.scalar.activation(sp_e[:, 0], a_par, ACT.Abs).then_inc(sp_abs, 1)
            act.wait_ge(sp_abs, 1)
            nc.scalar.activation(sp_e[:, 1], sp_e[:, 0], ACT.Exp, scale=-1.0).then_inc(sp_exp, 1)
            act.wait_ge(sp_exp, 1)
            nc.scalar.activation(sp_e[:, 2], sp_e[:, 1], ACT.Ln, bias=1.0).then_inc(sp_log, 1)
            for s in range(SEQS):
                act.wait_ge(v_set, s + 1)
                nc.scalar.activation(ln[:, LOG, s], ln[:, V, s], ACT.Ln).then_inc(log_set, 1)
                act.wait_ge(log_set, s + 1)
                nc.scalar.activation(ln[:, R0, s], ln[:, LOG, s], ACT.Exp, scale=-0.5).then_inc(r0_set, 1)
            square_hi(WX)

            def xt_hi_of(s):
                act.wait_ge(xt_psum, s + 1)
                nc.scalar.activation(xt_hi[:, s], slot[T_SLOT[s]][:, :, :], ACT.Copy).then_inc(xt_hi_set, 1)

            junk_a = tx[:, :, :, :].rearrange("p s c n -> p (s c n)")
            junk_b = ta[:, :, :, :].rearrange("p s c n -> p (s c n)")
            junk_c = g_hi[:, :, :, :].rearrange("p j s n -> p (j s n)")

            def abs_sum_of(src, chunks, junk, col, done):
                parts, n = src.shape[0], src.shape[-1]
                out = junk[0:parts, 0:chunks * n]
                if chunks > 1:
                    out = out.rearrange("p (c n) -> p c n", c=chunks)
                nc.scalar.activation(out, src, ACT.Abs, accum_out=abs_sum[0:parts, col:col + 1]).then_inc(done, 1)

            xt_hi_of(0)
            xt_hi_of(1)
            act.wait_ge(w1_loaded, 16)
            abs_sum_of(w13_raw[:, :, 0:HIDDEN], KC, junk_a, 0, abs13_set)
            act.wait_ge(w3_loaded, 16)
            abs_sum_of(w13_raw[:, :, W3_AT:W13], KC, junk_b, 1, abs13_set)
            square_hi(WY)

            def xb_of(s):
                act.wait_ge(pads_set, 1)
                act.wait_ge(xb_psum, s + 1)
                for c in range(KC):
                    nc.scalar.activation(xb[:, s, c, TAPS - 1:], slot[X_SLOT[s]][:, c], ACT.Identity,
                                         bias=par[:, B_X + c:B_X + c + 1]).then_inc(xb_set, 1)

            xb_of(0)
            act.wait_ge(w2_loaded, 48)
            act.wait_ge(consts_set, 3)
            abs_sum_of(w2_raw[:, 0:FULL, :], FULL, junk_c, 2, abs2_set)
            abs_sum_of(w2_raw[0:TAIL, FULL, :], 1, junk_c[:, FULL * D:], 3, abs2_set)
            xb_of(1)
            square_hi(WIG)
            square_hi(WAG)
            square_hi(WOUT)
            for s in range(SEQS):
                act.wait_ge(y_psum, s + 1)
                for c in range(KC):
                    nc.scalar.activation(y[:, s, c], slot[Y_SLOT[s]][:, c], ACT.Gelu,
                                         bias=par[:, B_Y + c:B_Y + c + 1]).then_inc(y_set, 1)

            def silu_of(n):
                s, j = HJ[n]
                act.wait_ge(h_psum, n + 1)
                if n >= RING:
                    act.wait_ge(g_set, n - RING + 1)
                nc.scalar.activation(silu[:, n % RING], slot[H_SLOT[s][j]][:, 0], ACT.Silu,
                                     scale=scale[:, 0:1]).then_inc(silu_set, 1)

            def g_hi_of(n):
                s, j = HJ[n]
                act.wait_ge(g_set, n + 1)
                nc.scalar.activation(g_hi[:, j, s], g[:, n % RING], ACT.Copy).then_inc(g_hi_set, 1)

            def conv_hi_of(s):
                act.wait_ge(conv_set, KC * (s + 1))
                nc.scalar.activation(conv_hi[:, s], conv[:, s], ACT.Copy).then_inc(conv_hi_set, 1)

            def gates(s):
                act.wait_ge(half_b_set, 1)
                act.wait_ge(gx_psum, s + 1)
                for c in range(KC):
                    nc.scalar.activation(tx[:, s, c], slot[GX_SLOT[s]][:, c], ACT.Tanh,
                                         scale=0.5, bias=half_b[:, c:c + 1]).then_inc(tx_set, 1)
                act.wait_ge(ga_psum, s + 1)
                for c in range(KC):
                    nc.scalar.activation(ta[:, s, c], slot[GA_SLOT[s]][:, c], ACT.Tanh,
                                         scale=0.5, bias=half_b[:, KC + c:KC + c + 1]).then_inc(ta_set, 1)

            act.wait_ge(w_lo_set, WIG + 1)
            silu_of(0)
            silu_of(1)
            g_hi_of(0)
            silu_of(2)
            conv_hi_of(0)
            g_hi_of(1)
            g_hi_of(2)
            conv_hi_of(1)
            gates(0)
            silu_of(3)
            silu_of(4)
            g_hi_of(3)
            g_hi_of(4)
            act.wait_ge(t_psum, 1)
            act.wait_ge(w_lo_set, WOUT + 1)
            nc.scalar.activation(silu_t[HALF:HALF + TAIL], slot[TAIL_SLOT][0:TAIL].rearrange("p s n -> p (s n)"), ACT.Silu,
                                 scale=scale[0:TAIL, 0:1]).then_inc(silu_t_set, 1)
            gates(1)
            act.wait_ge(g_t_set, 1)
            act.wait_ge(pads_set, 2)
            nc.scalar.activation(gt[0:TAIL].rearrange("p s n -> p (s n)"), g_t[HALF:HALF + TAIL], ACT.Copy).then_inc(gt_hi_set, 1)
            nc.scalar.activation(gt_hi[HALF:HALF + TAIL].rearrange("p s n -> p (s n)"), g_t[HALF:HALF + TAIL], ACT.Copy).then_inc(gt_hi_set, 1)
            act.wait_ge(rate_set, 2)
            for s in range(SEQS):
                for c in range(KC):
                    act.wait_ge(ta_set, KC * s + c + 1)
                    nc.scalar.activation(ta[:, s, c], ta[:, s, c], ACT.Exp, scale=a_rate[:, c:c + 1],
                                         bias=a_rate[:, c:c + 1]).then_inc(a_set, 1)
            for s in range(SEQS):
                act.wait_ge(a_set, KC * (s + 1))
                act.wait_ge(mult0_set, s + 1)
                nc.scalar.activation(xb[:, s, :, TAPS:], ta[:, s, :, 1:], ACT.Square).then_inc(a2_set, 1)
            act.wait_ge(quarter_set, 1)
            for s in range(SEQS):
                act.wait_ge(a2_set, s + 1)
                nc.scalar.activation(xb[:, s, :, TAPS:], xb[:, s, :, TAPS:], ACT.Sqrt, scale=-0.25, bias=quarter[:, 0:1]).then_inc(mult_set, 1)
            for n in range(FULL, 2 * FULL):
                silu_of(n)
                if n > FULL:
                    g_hi_of(n - 1)
                if n == FULL + 2:
                    act.wait_ge(hy_set, 1)
                    nc.scalar.activation(conv_hi[:, 0], tx[:, 0], ACT.Copy).then_inc(hy_hi_set, 1)
            g_hi_of(2 * FULL - 1)
            act.wait_ge(hy_set, 2)
            nc.scalar.activation(conv_hi[:, 1], tx[:, 1], ACT.Copy).then_inc(hy_hi_set, 1)

        @block.vector
        def _(dve):
            nc.vector.memset(quarter[:, :], 0.25).then_inc(quarter_set, 1)

            def statistics(s):
                dve.wait_ge(x_loaded[s], 16)
                for t in range(TILES):
                    nc.vector.bn_stats(stats[:, s, t], x_sb[:, s, t]).then_inc(stats_set, 1)
                for t in range(TILES):
                    dve.wait_ge(stats_set, TILES * s + t + 1)
                    nc.vector.bn_aggr(mv[:, s, t], stats[:, s, t]).then_inc(mv_set, 1)
                dve.wait_ge(mv_set, TILES * (s + 1))
                nc.vector.tensor_scalar(ln[:, V, s], mv[:, s, :, 1], EPS, None, ALU.add).then_inc(v_set, 1)

            def normalise(s):
                dve.wait_ge(r0_set, s + 1)
                k = 3 * s
                nc.vector.tensor_tensor(ln[:, SQ, s], ln[:, R0, s], ln[:, R0, s], ALU.mult).then_inc(rstd_step, 1)
                dve.wait_ge(rstd_step, k + 1)
                nc.vector.scalar_tensor_tensor(out=ln[:, VSQ, s], in0=ln[:, SQ, s], scalar=-0.5, in1=ln[:, V, s],
                                               op0=ALU.mult, op1=ALU.mult).then_inc(rstd_step, 1)
                dve.wait_ge(rstd_step, k + 2)
                nc.vector.scalar_tensor_tensor(out=ln[:, RSTD, s], in0=ln[:, VSQ, s], scalar=1.5, in1=ln[:, R0, s],
                                               op0=ALU.add, op1=ALU.mult).then_inc(rstd_step, 1)
                dve.wait_ge(rstd_step, k + 3)
                for t in range(TILES):
                    nc.vector.tensor_scalar(xn[:, s, t], x_sb[:, s, t], mv[:, s, t, 0:1], ln[:, RSTD, s, t:t + 1],
                                            ALU.subtract, ALU.mult).then_inc(xn_set, 1)

            def xt_lo_of(s):
                dve.wait_ge(xt_hi_set, s + 1)
                nc.vector.tensor_tensor(xt_lo[:, s], slot[T_SLOT[s]][:, :, :], xt_hi[:, s].bitcast(f32), ALU.subtract).then_inc(xt_lo_set, 1)

            statistics(0)
            normalise(0)
            statistics(1)
            normalise(1)
            dve.wait_ge(sp_log, 1)
            nc.vector.scalar_tensor_tensor(out=a_rate[:, :], in0=par[:, A_PARAM:A_PARAM + KC], scalar=0.0, in1=sp_e[:, 2],
                                           op0=ALU.max, op1=ALU.add).then_inc(rate_set, 1)
            nc.vector.tensor_scalar(half_b[:, :], par[:, B_IG:B_IG + 2 * KC], 0.5, None, ALU.mult).then_inc(half_b_set, 1)
            dve.wait_ge(rate_set, 1)
            nc.vector.tensor_scalar(a_rate[:, :], a_rate[:, :], -4.0, None, ALU.mult).then_inc(rate_set, 1)
            xt_lo_of(0)
            xt_lo_of(1)

            dve.wait_ge(sum13_psum, 1)
            nc.vector.tensor_scalar(thr[:, 0], sums[:, 0:2], 0.5 / WEIGHTS, None, ALU.mult).then_inc(thr_set, 1)
            nc.vector.tensor_scalar(thr[:, 1], sums[:, 0:2], -0.5 / WEIGHTS, None, ALU.mult).then_inc(thr_set, 1)
            nc.vector.tensor_scalar(scale[:, 0:2], sums[:, 0:2], 1.0 / WEIGHTS, None, ALU.mult).then_inc(thr_set, 1)
            dve.wait_ge(thr_set, 2)
            dve.wait_ge(gaps_set, 1)
            parts = (slice(0, W3_AT), slice(W3_AT, W13))
            for i, cols in enumerate(parts):
                nc.vector.tensor_scalar(below[:, :, cols], w13_raw[:, :, cols], thr[:, 1, i:i + 1], None, ALU.is_lt).then_inc(below_set, 1)
            for i, cols in enumerate(parts):
                dve.wait_ge(below_set, i + 1)
                nc.vector.scalar_tensor_tensor(out=w13_q[:, :, cols], in0=w13_raw[:, :, cols], scalar=thr[:, 0, i:i + 1],
                                               in1=below[:, :, cols], op0=ALU.is_gt, op1=ALU.subtract).then_inc(w13_q_set, 1)
            dve.wait_ge(sum2_psum, 1)
            nc.vector.tensor_scalar(scale[:, 2:3], sums[:, 2:3], 1.0 / WEIGHTS, None, ALU.mult).then_inc(s2_ready, 1)
            dve.wait_ge(s2_ready, 1)
            dve.wait_ge(thr_set, 3)
            nc.vector.reciprocal(inv_s2[:, :], scale[:, 2:3]).then_inc(scale2_set, 1)
            nc.vector.tensor_tensor(s32[:, :], scale[:, 1:2], scale[:, 2:3], ALU.mult).then_inc(scale2_set, 1)

            def convolve(s):
                for i in range(1, TAPS):
                    k = TAPS - 1 - i
                    for c in range(KC):
                        if i == 1:
                            dve.wait_ge(tap_set, KC * s + c + 1)
                        else:
                            dve.wait_ge(tap_step, KC * (TAPS - 2) * s + KC * (i - 2) + c + 1)
                        nc.vector.scalar_tensor_tensor(
                            out=conv[:, s, c], in0=xb[:, s, c, k:k + SEQ],
                            scalar=par[:, CONV_W + KC * k + c:CONV_W + KC * k + c + 1],
                            in1=conv[:, s, c], op0=ALU.mult, op1=ALU.add).then_inc(conv_set if i == TAPS - 1 else tap_step, 1)
                dve.wait_ge(conv_set, KC * (s + 1))
                nc.vector.memset(xb[:, s, :, TAPS - 1:TAPS], 0.5).then_inc(mult0_set, 1)

            def g_of(n):
                s, j = HJ[n]
                if n == 0:
                    dve.wait_ge(scale2_set, 2)
                dve.wait_ge(silu_set, n + 1)
                if n >= RING:
                    dve.wait_ge(g_lo_set, n - RING + 1)
                nc.vector.scalar_tensor_tensor(out=g[:, n % RING], in0=silu[:, n % RING], scalar=s32[:, 0:1],
                                               in1=slot[H_SLOT[s][j]][:, 1], op0=ALU.mult, op1=ALU.mult).then_inc(g_set, 1)

            def gated_input(s):
                dve.wait_ge(tx_set, KC * (s + 1))
                nc.vector.scalar_tensor_tensor(out=tx[:, s], in0=tx[:, s], scalar=1.0, in1=conv[:, s],
                                               op0=ALU.add, op1=ALU.mult).then_inc(nx_step, 1)

            def recurrence(s):
                dve.wait_ge(mult_set, s + 1)
                dve.wait_ge(nx_step, s + 1)
                nc.vector.tensor_tensor(tx[:, s], tx[:, s], xb[:, s, :, TAPS - 1:], ALU.mult).then_inc(nx_set, 1)
                dve.wait_ge(nx_set, s + 1)
                for c in range(KC):
                    nc.vector.tensor_tensor_scan(tx[:, s, c], ta[:, s, c], tx[:, s, c], 0.0, ALU.mult, ALU.add).then_inc(h_set, 1)
                dve.wait_ge(h_set, KC * (s + 1))
                dve.wait_ge(y_set, KC * (s + 1))
                nc.vector.tensor_tensor(tx[:, s], tx[:, s], y[:, s], ALU.mult).then_inc(hy_set, 1)

            def lo_of_hy(s):
                dve.wait_ge(hy_hi_set, s + 1)
                nc.vector.tensor_tensor(conv_lo[:, s], tx[:, s], conv_hi[:, s].bitcast(f32), ALU.subtract).then_inc(hy_lo_set, 1)

            def output(s):
                for i in range(2):
                    dve.wait_ge(o_psum, 2 * s + i + 1)
                    dve.wait_ge(x_res_set, TILES * (s + 1))
                    t = slice(i * TILES // 2, (i + 1) * TILES // 2)
                    nc.vector.tensor_tensor(x_sb[:, s, t], slot[O_SLOT[s]][:, i].rearrange("p (t d) -> p t d", d=D), x_sb[:, s, t], ALU.add).then_inc(o_set, 1)

            convolve(0)
            g_of(0)
            g_of(1)
            convolve(1)
            g_of(2)
            gated_input(0)
            g_of(3)
            g_of(4)
            dve.wait_ge(silu_t_set, 1)
            nc.vector.scalar_tensor_tensor(out=g_t[HALF:HALF + TAIL], in0=silu_t[HALF:HALF + TAIL], scalar=s32[HALF:HALF + TAIL, 0:1],
                                           in1=slot[TAIL_SLOT][HALF:HALF + TAIL].rearrange("p s n -> p (s n)"), op0=ALU.mult, op1=ALU.mult).then_inc(g_t_set, 1)
            gated_input(1)
            dve.wait_ge(gt_hi_set, 2)
            nc.vector.tensor_tensor(gt[HALF:HALF + TAIL].rearrange("p s n -> p (s n)"), g_t[HALF:HALF + TAIL],
                                    gt_hi[HALF:HALF + TAIL].rearrange("p s n -> p (s n)").bitcast(f32), ALU.subtract).then_inc(gt_lo_set, 1)
            recurrence(0)
            g_of(5)
            g_of(6)
            recurrence(1)
            g_of(7)
            lo_of_hy(0)
            g_of(8)
            g_of(9)
            lo_of_hy(1)
            output(0)
            output(1)

        @block.tensor
        def _(pe):
            def transposes(s):
                for t in range(TILES):
                    pe.wait_ge(xn_set, TILES * s + t + 1)
                    for c in range(KC):
                        mm = nc.tensor.transpose(slot[T_SLOT[s]][:, c, t * P:(t + 1) * P], xn[:, s, t, c * P:(c + 1) * P], ident[:, :])
                mm.then_inc(xt_psum, 1)

            def dense_product(dst, m, hi, lo, done):
                for o in range(KC):
                    cols = slice(o * P, (o + 1) * P)
                    terms = [(w_hi, hi), (w_hi, lo), (w_lo, hi)]
                    for i, (w, v) in enumerate(terms):
                        for c in range(KC):
                            mm = nc.tensor.matmul(dst[:, o], w[:, m, c, cols], v[:, c], start=(i == 0 and c == 0),
                                                  stop=(i == len(terms) - 1 and c == KC - 1))
                mm.then_inc(done, 1)

            def hidden(n):
                s, j = HJ[n]
                for o, col in enumerate((j * P, W3_AT + TAIL + j * P)):
                    for c in range(KC):
                        for v in (xt_hi, xt_lo):
                            mm = nc.tensor.matmul(slot[H_SLOT[s][j]][:, o], w13_q[:, c, col:col + P], v[:, s, c],
                                                  start=(c == 0 and v is xt_hi), stop=(c == KC - 1 and v is xt_lo))
                mm.then_inc(h_psum, 1)

            def hidden_tail():
                for s in range(SEQS):
                    for c in range(KC):
                        for v in (xt_hi, xt_lo):
                            mm = nc.tensor.matmul(slot[TAIL_SLOT][:, s], w13_q[:, c, FULL * P:(FULL + 1) * P], v[:, s, c],
                                                  start=(c == 0 and v is xt_hi), stop=(c == KC - 1 and v is xt_lo))
                mm.then_inc(t_psum, 1)

            def out_tile(s, t):
                return slot[O_SLOT[s]][:, t // 2, (t % 2) * D:(t % 2 + 1) * D]

            def down(s):
                for j in range(FULL + 1):
                    if j < FULL:
                        pe.wait_ge(g_lo_set, FULL * s + j + 1)
                    else:
                        pe.wait_ge(gt_lo_set, 1)
                    for t in range(TILES):
                        rows = slice(t * P, (t + 1) * P)
                        if j < FULL:
                            for v in (g_hi, g_lo):
                                nc.tensor.matmul(out_tile(s, t), v[:, j, s, rows], w2_q[:, j], start=(j == 0 and t % 2 == 0 and v is g_hi),
                                                 stop=False, skip_group_check=True)
                        else:
                            nc.tensor.matmul(out_tile(s, t), gt[:, s, rows], w2_q[:, j], start=False, stop=False, skip_group_check=True)

            def project(s):
                pe.wait_ge(w_lo_set, WOUT + 1)
                pe.wait_ge(hy_lo_set, s + 1)
                for t in range(TILES):
                    rows = slice(t * P, (t + 1) * P)
                    terms = [(conv_hi, w_hi), (conv_lo, w_hi), (conv_hi, w_lo)]
                    for i, (v, w) in enumerate(terms):
                        for c in range(KC):
                            mm = nc.tensor.matmul(out_tile(s, t), v[:, s, c, rows], w[:, WOUT, c], start=False,
                                                  stop=(i == len(terms) - 1 and c == KC - 1), skip_group_check=True)
                    if t % 2:
                        mm.then_inc(o_psum, 1)

            pe.wait_ge(ident_set, 1)
            transposes(0)
            transposes(1)
            for s in range(SEQS):
                pe.wait_ge(w_lo_set, WX + 1)
                pe.wait_ge(xt_lo_set, s + 1)
                dense_product(slot[X_SLOT[s]], WX, xt_hi[:, s], xt_lo[:, s], xb_psum)
            pe.wait_ge(consts_set, 3)
            pe.wait_ge(abs13_set, 2)
            pe.wait_ge(xb_set, KC)
            nc.tensor.matmul(sums[:, 0:2], ones[:, :], abs_sum[:, 0:2], start=True, stop=True).then_inc(sum13_psum, 1)
            pe.wait_ge(w_lo_set, WY + 1)
            dense_product(slot[Y_SLOT[0]], WY, xt_hi[:, 0], xt_lo[:, 0], y_psum)
            pe.wait_ge(abs2_set, 2)
            pe.wait_ge(thr_set, 3)
            for i in range(2):
                mm = nc.tensor.matmul(sums[:, 2:3], ones[:, :], abs_sum[:, 2 + i:3 + i], start=(i == 0), stop=(i == 1))
            mm.then_inc(sum2_psum, 1)
            dense_product(slot[Y_SLOT[1]], WY, xt_hi[:, 1], xt_lo[:, 1], y_psum)
            pe.wait_ge(w13_q_set, 2)
            pe.wait_ge(scale2_set, 2)
            hidden(0)
            pe.wait_ge(xb_set, 2 * KC)
            hidden(1)
            pe.wait_ge(y_set, KC)
            hidden(2)
            pe.wait_ge(w_lo_set, WAG + 1)

            def gate_products(s):
                pe.wait_ge(conv_lo_set, s + 1)
                if s == 0:
                    pe.wait_ge(y_set, 2 * KC)
                else:
                    pe.wait_ge(ta_set, KC)
                dense_product(slot[GX_SLOT[s]], WIG, conv_hi[:, s], conv_lo[:, s], gx_psum)
                pe.wait_ge(g_set, 1 if s == 0 else 4)
                dense_product(slot[GA_SLOT[s]], WAG, conv_hi[:, s], conv_lo[:, s], ga_psum)

            gate_products(0)
            pe.wait_ge(g_set, 2)
            hidden(3)
            pe.wait_ge(g_set, 3)
            hidden(4)
            pe.wait_ge(tx_set, KC)
            hidden_tail()
            gate_products(1)
            pe.wait_ge(g_set, 5)
            pe.wait_ge(w2_q_set, 1)
            down(0)
            pe.wait_ge(g_t_set, 1)
            hidden(5)
            pe.wait_ge(tx_set, 2 * KC)
            hidden(6)
            pe.wait_ge(ta_set, 2 * KC)
            hidden(7)
            pe.wait_ge(g_set, 6)
            hidden(8)
            pe.wait_ge(g_set, 7)
            hidden(9)
            project(0)
            pe.wait_ge(g_set, 8)
            down(1)
            project(1)


def kernel(L0_attn_x, L0_attn_w_y, L0_attn_b_y, L0_attn_w_x, L0_attn_b_x, L0_attn_conv_w, L0_attn_conv_b,
           L0_attn_a_param, L0_attn_w_ig, L0_attn_b_ig, L0_attn_w_ag, L0_attn_b_ag, L0_attn_w_out, L0_attn_b_out,
           L0_ffn_w1, L0_ffn_w3, L0_ffn_w2):
    import numpy as np
    import concourse.bacc as bacc
    from concourse.bass_utils import run_bass_kernel_spmd

    x = np.ascontiguousarray(L0_attn_x)
    w3t = np.asarray(L0_ffn_w3).T
    vectors = [L0_attn_b_y, L0_attn_b_x, L0_attn_conv_b, L0_attn_a_param, L0_attn_b_ig, L0_attn_b_ag, *L0_attn_conv_w]
    arrays = {
        "x": x.reshape(TOKENS, D),
        "dense": np.stack([L0_attn_w_x, L0_attn_w_y, L0_attn_w_ig, L0_attn_w_ag, L0_attn_w_out]),
        "w13t": np.concatenate([np.asarray(L0_ffn_w1).T, w3t[:, FULL * P:], w3t[:, :FULL * P]], axis=1),
        "w2t": np.asarray(L0_ffn_w2).T,
        "params": np.stack(vectors).reshape(len(vectors) * KC, P).T,
        "b_out": np.asarray(L0_attn_b_out),
    }
    arrays = {k: np.ascontiguousarray(v) for k, v in arrays.items()}
    nc = bacc.Bacc("TRN2", target_bir_lowering=False, num_devices=1)
    aps = [nc.dram_tensor(k, v.shape, mybir.dt.from_np(v.dtype), kind="ExternalInput").ap() for k, v in arrays.items()]
    out = nc.dram_tensor("out", (TOKENS, D), mybir.dt.float32, kind="ExternalOutput").ap()
    build(nc, *aps, out)
    result = run_bass_kernel_spmd(nc, [arrays], core_ids=[0])
    return result.results[0]["out"].reshape(x.shape)
```

```python
from contextlib import ExitStack

import concourse.bass as bass
from concourse import mybir

P = 128
SEQS, SEQ = 2, 512
TOKENS = SEQS * SEQ
D = 256
HIDDEN = 682
TAPS = 4
KC = D // P
TILES = SEQ // P
FULL = HIDDEN // P
TAIL = HIDDEN - FULL * P
HALF = 64
W3_AT = FULL * P + HALF
W13 = W3_AT + HIDDEN
EPS = 1e-5
WEIGHTS = D * HIDDEN

B_Y, B_X, CONV_B, A_PARAM, B_IG, B_AG, CONV_W = (KC * i for i in range(7))
PARAMS = CONV_W + KC * TAPS
WX, WY, WIG, WAG, WOUT = range(5)


def build(nc: bass.Bass, x, dense, w13t, w2t, params, b_out, out):
    f32, f32r, bf16 = mybir.dt.float32, mybir.dt.float32r, mybir.dt.bfloat16
    ALU, ACT = mybir.AluOpType, mybir.ActivationFunctionType

    x_dram = x.rearrange("(s t p) d -> s p t d", s=SEQS, p=P)
    out_dram = out.rearrange("(s t p) d -> s p t d", s=SEQS, p=P)

    ctx = ExitStack()
    with ctx:
        def sb(name, shape, dt=f32):
            return ctx.enter_context(nc.sbuf_tensor(name, shape, dt))

        def sem(name):
            return ctx.enter_context(nc.semaphore(name))

        x_sb = sb("x_sb", [P, SEQS, TILES, D])
        xn_y = sb("xn_y", [P, SEQS * TILES * D])
        xn = xn_y[:, :].rearrange("p (s t d) -> p s t d", s=SEQS, t=TILES)
        y = xn_y[:, :].rearrange("p (s c n) -> p s c n", s=SEQS, c=KC)
        xt_hi = sb("xt_hi", [P, SEQS, KC, SEQ], f32r)
        xt_lo = sb("xt_lo", [P, SEQS, KC, SEQ], f32r)
        w_raw = sb("w_raw", [P, 5, KC, D])
        w_hi = sb("w_hi", [P, 5, KC, D], f32r)
        w_lo = sb("w_lo", [P, 5, KC, D], f32r)
        w13_raw = sb("w13_raw", [P, KC, W13])
        w13_q = sb("w13_q", [P, KC, W13], f32r)
        below = sb("below", [P, KC, W13], bf16)
        w2_raw = sb("w2_raw", [P, FULL + 1, D])
        w2_q = sb("w2_q", [P, FULL + 1, D], f32r)
        xb = sb("xb", [P, SEQS, KC, TAPS - 1 + SEQ])
        conv = sb("conv", [P, SEQS, KC, SEQ])
        conv_hi = sb("conv_hi", [P, SEQS, KC, SEQ], f32r)
        conv_lo = sb("conv_lo", [P, SEQS, KC, SEQ], f32r)
        tx = sb("tx", [P, SEQS, KC, SEQ])
        ta = sb("ta", [P, SEQS, KC, SEQ])
        g_hi = sb("g_hi", [P, FULL, SEQS, SEQ], f32r)
        g_lo = sb("g_lo", [P, FULL, SEQS, SEQ], f32r)
        gt = sb("gt", [P, SEQS, SEQ], f32r)
        gt_hi = sb("gt_hi", [P, SEQS, SEQ], f32r)
        RING = 3
        par = sb("par", [P, PARAMS])
        half_b = sb("half_b", [P, 2 * KC])
        a_rate = sb("a_rate", [P, KC])
        sp_e = sb("sp_e", [P, 3, KC])
        b_out_bc = sb("b_out_bc", [P, D])
        ident = sb("ident", [P, P])
        ones = sb("ones", [P, P])
        stats = sb("stats", [P, SEQS, TILES, 6])
        mv = sb("mv", [P, SEQS, TILES, 2])
        ln = sb("ln", [P, 6, SEQS, TILES])
        V, ROOT, R0, SQ, VSQ, RSTD = range(6)
        abs_sum = sb("abs_sum", [P, 4])
        thr = sb("thr", [P, 2, 2])
        scale = sb("scale", [P, 3])
        thr2 = sb("thr2", [P, 2])
        quarter = sb("quarter", [P, 1])
        s32 = sb("s32", [P, 1])

        w_flat = w_raw[:, :, :, :].rearrange("p m c n -> p (m c n)")
        silu = w_flat[:, 0:RING * SEQ].rearrange("p (r n) -> p r n", r=RING)
        silu_t = w_flat[:, RING * SEQ:RING * SEQ + TOKENS]
        w13_flat = w13_raw[:, :, :].rearrange("p c n -> p (c n)")
        g = w13_flat[:, 0:RING * SEQ].rearrange("p (r n) -> p r n", r=RING)
        g_t = w13_flat[:, RING * SEQ:RING * SEQ + TOKENS]

        slot = [ctx.enter_context(nc.psum_tensor(f"slot{i}", [P, 2, SEQ], f32)) for i in range(4)]
        T_SLOT, X_SLOT, Y_SLOT = (0, 1), (2, 3), (0, 1)
        H_SLOT = ((2, 3, 0, 3, 0), (1, 0, 3, 1, 0))
        TAIL_SLOT = 1
        GX_SLOT, GA_SLOT = (1, 2), (2, 3)
        O_SLOT = (2, 3)
        sums13 = slot[3][:, 0, 0:2]
        sum2 = slot[2][:, 0, 0:1]

        x_loaded = [sem(f"x_loaded{i}") for i in range(3)]
        w_loaded = [sem(f"w_loaded{m}") for m in range(5)]
        w1_loaded, w3_loaded = sem("w1_loaded"), sem("w3_loaded")
        w2_loaded = sem("w2_loaded")
        par_loaded, b_out_loaded = sem("par_loaded"), sem("b_out_loaded")
        out_stored = sem("out_stored")
        consts_set, ident_set, pads_set = sem("consts_set"), sem("ident_set"), sem("pads_set")
        quarter_set = sem("quarter_set")
        gaps_set = sem("gaps_set")
        stats_set, mv_set, v_set = sem("stats_set"), sem("mv_set"), sem("v_set")
        root_set, r0_set, rstd_step = sem("root_set"), sem("r0_set"), sem("rstd_step")
        xn_set, xt_psum, xt_hi_set, xt_lo_set = sem("xn_set"), sem("xt_psum"), sem("xt_hi_set"), sem("xt_lo_set")
        w_hi_set = sem("w_hi_set")
        w_lo_set = sem("w_lo_set")
        sp_abs, sp_exp, sp_log, sp_relu, rate_set, half_b_set = (
            sem("sp_abs"), sem("sp_exp"), sem("sp_log"), sem("sp_relu"), sem("rate_set"), sem("half_b_set"))
        abs13_set, abs2_set, sum13_psum, sum2_psum = (
            sem("abs13_set"), sem("abs2_set"), sem("sum13_psum"), sem("sum2_psum"))
        thr_set, scale2_set, s2_ready = sem("thr_set"), sem("scale2_set"), sem("s2_ready")
        below_set, w13_q_set, w2_q_set = sem("below_set"), sem("w13_q_set"), sem("w2_q_set")
        xb_psum, xb_set = sem("xb_psum"), sem("xb_set")
        tap_set, tap_step, conv_set = sem("tap_set"), sem("tap_step"), sem("conv_set")
        conv_hi_set, conv_lo_set = sem("conv_hi_set"), sem("conv_lo_set")
        y_psum, y_set = sem("y_psum"), sem("y_set")
        gx_psum, ga_psum, tx_set, ta_set = sem("gx_psum"), sem("ga_psum"), sem("tx_set"), sem("ta_set")
        a_set, a2_set, mult_set, mult0_set = sem("a_set"), sem("a2_set"), sem("mult_set"), sem("mult0_set")
        nx_step, nx_set, h_set, hy_set = sem("nx_step"), sem("nx_set"), sem("h_set"), sem("hy_set")
        hy_hi_set, hy_lo_set = sem("hy_hi_set"), sem("hy_lo_set")
        h_psum, silu_set, g_set, g_hi_set, g_lo_set = (
            sem("h_psum"), sem("silu_set"), sem("g_set"), sem("g_hi_set"), sem("g_lo_set"))
        t_psum, silu_t_set, g_t_set, gt_hi_set, gt_lo_set = (
            sem("t_psum"), sem("silu_t_set"), sem("g_t_set"), sem("gt_hi_set"), sem("gt_lo_set"))
        x_res_set, o_psum, o_set = sem("x_res_set"), sem("o_psum"), sem("o_set")

        HJ = [(s, j) for s in range(SEQS) for j in range(FULL)]

        block = ctx.enter_context(nc.Block())

        @block.sync
        def _(sp):
            def square(m):
                sp.dma_start(w_raw[:, m], dense[m].rearrange("(c p) n -> p c n", p=P)).then_inc(w_loaded[m], 16)

            for i in range(2):
                t = slice(i * TILES // 2, (i + 1) * TILES // 2)
                sp.dma_start(x_sb[:, 0, t], x_dram[0][:, t]).then_inc(x_loaded[i], 16)
            square(WX)
            sp.dma_start(x_sb[:, 1], x_dram[1]).then_inc(x_loaded[2], 16)
            w13_dram = w13t.rearrange("(c p) n -> p c n", p=P)
            sp.dma_start(w13_raw[:, :, 0:HIDDEN], w13_dram[:, :, 0:HIDDEN]).then_inc(w1_loaded, 16)
            sp.dma_start(w13_raw[:, :, W3_AT:W13], w13_dram[:, :, HIDDEN:2 * HIDDEN]).then_inc(w3_loaded, 16)
            square(WY)
            sp.dma_start(w2_raw[:, 0:FULL], w2t[0:FULL * P].rearrange("(j p) n -> p j n", p=P)).then_inc(w2_loaded, 16)
            sp.wait_ge(gaps_set, 2)
            sp.dma_start(w2_raw[0:TAIL, FULL], w2t[FULL * P:HIDDEN]).then_inc(w2_loaded, 16)
            sp.dma_start(w2_raw[HALF:HALF + TAIL, FULL], w2t[FULL * P:HIDDEN]).then_inc(w2_loaded, 16)
            square(WIG)
            square(WAG)
            square(WOUT)
            for s in range(SEQS):
                for i in range(2):
                    sp.wait_ge(o_set, 2 * s + i + 1)
                    t = slice(i * TILES // 2, (i + 1) * TILES // 2)
                    sp.dma_start(out_dram[s][:, t], x_sb[:, s, t]).then_inc(out_stored, 16)
            sp.wait_ge(out_stored, 16 * 2 * SEQS)

        @block.gpsimd
        def _(pool):
            nc.gpsimd.memset(ident[:, :], 0.0).then_inc(consts_set, 1)
            nc.gpsimd.memset(w13_raw[:, :, HIDDEN:W3_AT], 0.0).then_inc(gaps_set, 1)
            nc.gpsimd.memset(w2_raw[:, FULL, :], 0.0).then_inc(gaps_set, 1)
            pool.wait_ge(consts_set, 1)
            nc.gpsimd.affine_select(out=ident[:, :], in_=ident[:, :], compare_op=ALU.not_equal, fill=1.0, base=0,
                                    pattern=[[-1, P]], channel_multiplier=1).then_inc(ident_set, 1)
            nc.gpsimd.memset(ones[:, :], 1.0).then_inc(consts_set, 1)
            nc.gpsimd.memset(abs_sum[:, 3:4], 0.0).then_inc(consts_set, 1)
            nc.gpsimd.memset(xb[:, :, :, 0:TAPS - 1], 0.0).then_inc(pads_set, 1)
            nc.gpsimd.memset(gt[:, :, :].bitcast(f32), 0.0).then_inc(pads_set, 1)

            def square_lo(m):
                pool.wait_ge(w_hi_set, m + 1)
                nc.gpsimd.tensor_tensor(w_lo[:, m], w_raw[:, m], w_hi[:, m].bitcast(f32), ALU.subtract).then_inc(w_lo_set, 1)

            def newest_tap(s):
                for c in range(KC):
                    pool.wait_ge(xb_set, KC * s + c + 1)
                    k = TAPS - 1
                    nc.gpsimd.tensor_scalar(conv[:, s, c], xb[:, s, c, k:k + SEQ],
                                            par[:, CONV_W + KC * k + c:CONV_W + KC * k + c + 1],
                                            par[:, CONV_B + c:CONV_B + c + 1], ALU.mult, ALU.add).then_inc(tap_set, 1)

            def residual(s):
                pool.wait_ge(xn_set, TILES * (s + 1))
                pool.wait_ge(b_out_loaded, 16)
                for t in range(TILES):
                    nc.gpsimd.tensor_tensor(x_sb[:, s, t], x_sb[:, s, t], b_out_bc[:, :], ALU.add).then_inc(x_res_set, 1)

            def lo_of_conv(s):
                for c in range(KC):
                    pool.wait_ge(conv_hi_set, KC * s + c + 1)
                    nc.gpsimd.tensor_tensor(conv_lo[:, s, c], conv[:, s, c], conv_hi[:, s, c].bitcast(f32), ALU.subtract).then_inc(conv_lo_set, 1)

            def lo_of_g(n):
                s, j = HJ[n]
                pool.wait_ge(g_hi_set, n + 1)
                nc.gpsimd.tensor_tensor(g_lo[:, j, s], g[:, n % RING], g_hi[:, j, s].bitcast(f32), ALU.subtract).then_inc(g_lo_set, 1)

            square_lo(WX)
            square_lo(WY)
            pool.wait_ge(par_loaded, 16)
            newest_tap(0)
            newest_tap(1)
            square_lo(WIG)
            square_lo(WAG)
            square_lo(WOUT)
            lo_of_conv(0)
            lo_of_conv(1)
            lo_of_g(0)
            lo_of_g(1)
            lo_of_g(2)
            lo_of_g(3)
            lo_of_g(4)
            residual(0)
            residual(1)
            for n in range(FULL, 2 * FULL):
                lo_of_g(n)

        @block.scalar
        def _(act):
            act.dma_start(par[:, :], params).then_inc(par_loaded, 16)
            act.dma_start(b_out_bc[:, :], b_out.partition_broadcast(P)).then_inc(b_out_loaded, 16)

            def square_hi(m):
                act.wait_ge(w_loaded[m], 16)
                nc.scalar.activation(w_hi[:, m], w_raw[:, m], ACT.Copy).then_inc(w_hi_set, 1)

            def root_of(s):
                act.wait_ge(v_set, s + 1)
                nc.scalar.activation(ln[:, ROOT, s], ln[:, V, s], ACT.Sqrt).then_inc(root_set, 1)

            def xt_hi_of(s):
                for c in range(KC):
                    act.wait_ge(xt_psum, KC * s + c + 1)
                    nc.scalar.activation(xt_hi[:, s, c], slot[T_SLOT[s]][:, c], ACT.Copy).then_inc(xt_hi_set, 1)

            junk_a = tx[:, :, :, :].rearrange("p s c n -> p (s c n)")
            junk_b = ta[:, :, :, :].rearrange("p s c n -> p (s c n)")
            junk_c = g_hi[:, :, :, :].rearrange("p j s n -> p (j s n)")

            def abs_sum_of(src, chunks, junk, col, done):
                parts, n = src.shape[0], src.shape[-1]
                out = junk[0:parts, 0:chunks * n]
                if chunks > 1:
                    out = out.rearrange("p (c n) -> p c n", c=chunks)
                nc.scalar.activation(out, src, ACT.Abs, accum_out=abs_sum[0:parts, col:col + 1]).then_inc(done, 1)

            root_of(0)
            square_hi(WX)
            xt_hi_of(0)
            root_of(1)
            act.wait_ge(w1_loaded, 16)
            abs_sum_of(w13_raw[:, :, 0:HIDDEN], KC, junk_a, 0, abs13_set)
            act.wait_ge(w3_loaded, 16)
            abs_sum_of(w13_raw[:, :, W3_AT:W13], KC, junk_b, 1, abs13_set)
            xt_hi_of(1)
            square_hi(WY)

            def xb_of(s):
                act.wait_ge(pads_set, 1)
                act.wait_ge(xb_psum, s + 1)
                for c in range(KC):
                    nc.scalar.activation(xb[:, s, c, TAPS - 1:], slot[X_SLOT[s]][:, c], ACT.Identity,
                                         bias=par[:, B_X + c:B_X + c + 1]).then_inc(xb_set, 1)

            act.wait_ge(par_loaded, 16)
            a_par = par[:, A_PARAM:A_PARAM + KC]
            nc.scalar.activation(sp_e[:, 0], a_par, ACT.Abs).then_inc(sp_abs, 1)
            act.wait_ge(sp_abs, 1)
            nc.scalar.activation(sp_e[:, 1], sp_e[:, 0], ACT.Exp, scale=-1.0).then_inc(sp_exp, 1)
            act.wait_ge(sp_exp, 1)
            nc.scalar.activation(sp_e[:, 2], sp_e[:, 1], ACT.Ln, bias=1.0).then_inc(sp_log, 1)
            xb_of(0)
            act.wait_ge(w2_loaded, 48)
            act.wait_ge(consts_set, 3)
            abs_sum_of(w2_raw[:, 0:FULL, :], FULL, junk_c, 2, abs2_set)
            abs_sum_of(w2_raw[0:TAIL, FULL, :], 1, junk_c[:, FULL * D:], 3, abs2_set)
            xb_of(1)
            square_hi(WIG)
            square_hi(WAG)
            square_hi(WOUT)
            def gelu_of(s):
                act.wait_ge(y_psum, s + 1)
                for c in range(KC):
                    nc.scalar.activation(y[:, s, c], slot[Y_SLOT[s]][:, c], ACT.Gelu,
                                         bias=par[:, B_Y + c:B_Y + c + 1]).then_inc(y_set, 1)

            def silu_of(n):
                s, j = HJ[n]
                act.wait_ge(h_psum, n + 1)
                if n >= RING:
                    act.wait_ge(g_set, n - RING + 1)
                nc.scalar.activation(silu[:, n % RING], slot[H_SLOT[s][j]][:, 0], ACT.Silu,
                                     scale=scale[:, 0:1]).then_inc(silu_set, 1)

            def g_hi_of(n):
                s, j = HJ[n]
                act.wait_ge(g_set, n + 1)
                nc.scalar.activation(g_hi[:, j, s], g[:, n % RING], ACT.Copy).then_inc(g_hi_set, 1)

            def conv_hi_of(s):
                for c in range(KC):
                    act.wait_ge(conv_set, KC * s + c + 1)
                    nc.scalar.activation(conv_hi[:, s, c], conv[:, s, c], ACT.Copy).then_inc(conv_hi_set, 1)

            def gates(s):
                act.wait_ge(half_b_set, 1)
                act.wait_ge(gx_psum, s + 1)
                for c in range(KC):
                    nc.scalar.activation(tx[:, s, c], slot[GX_SLOT[s]][:, c], ACT.Tanh,
                                         scale=0.5, bias=half_b[:, c:c + 1]).then_inc(tx_set, 1)
                act.wait_ge(ga_psum, s + 1)
                for c in range(KC):
                    nc.scalar.activation(ta[:, s, c], slot[GA_SLOT[s]][:, c], ACT.Tanh,
                                         scale=0.5, bias=half_b[:, KC + c:KC + c + 1]).then_inc(ta_set, 1)

            gelu_of(0)
            conv_hi_of(0)
            gelu_of(1)
            act.wait_ge(w_lo_set, WIG + 1)
            silu_of(0)
            silu_of(1)
            conv_hi_of(1)
            silu_of(2)
            g_hi_of(0)
            g_hi_of(1)
            g_hi_of(2)
            gates(0)
            silu_of(3)
            silu_of(4)
            g_hi_of(3)
            g_hi_of(4)
            act.wait_ge(t_psum, 1)
            act.wait_ge(w_lo_set, WOUT + 1)
            nc.scalar.activation(silu_t[HALF:HALF + TAIL], slot[TAIL_SLOT][0:TAIL].rearrange("p s n -> p (s n)"), ACT.Silu,
                                 scale=scale[0:TAIL, 0:1]).then_inc(silu_t_set, 1)
            gates(1)
            def hy_hi_of(s):
                act.wait_ge(hy_set, s + 1)
                nc.scalar.activation(conv_hi[:, s], tx[:, s], ACT.Copy).then_inc(hy_hi_set, 1)

            silu_of(5)
            silu_of(6)
            g_hi_of(5)
            act.wait_ge(rate_set, 2)
            for s in range(SEQS):
                for c in range(KC):
                    act.wait_ge(ta_set, KC * s + c + 1)
                    nc.scalar.activation(ta[:, s, c], ta[:, s, c], ACT.Exp, scale=a_rate[:, c:c + 1],
                                         bias=a_rate[:, c:c + 1]).then_inc(a_set, 1)
            act.wait_ge(quarter_set, 1)
            for s in range(SEQS):
                act.wait_ge(a2_set, s + 1)
                nc.scalar.activation(xb[:, s, :, TAPS:], xb[:, s, :, TAPS:], ACT.Sqrt, scale=-0.25, bias=quarter[:, 0:1]).then_inc(mult_set, 1)
            silu_of(7)
            g_hi_of(6)
            silu_of(8)
            silu_of(9)
            g_hi_of(7)
            g_hi_of(8)
            hy_hi_of(0)
            g_hi_of(9)
            hy_hi_of(1)

        @block.vector
        def _(dve):
            nc.vector.memset(quarter[:, :], 0.25).then_inc(quarter_set, 1)

            def statistics(s, tiles):
                for t in tiles:
                    nc.vector.bn_stats(stats[:, s, t], x_sb[:, s, t]).then_inc(stats_set, 1)

            def variance(s):
                for t in range(TILES):
                    dve.wait_ge(stats_set, TILES * s + t + 1)
                    nc.vector.bn_aggr(mv[:, s, t], stats[:, s, t]).then_inc(mv_set, 1)
                dve.wait_ge(mv_set, TILES * (s + 1))
                nc.vector.tensor_scalar(ln[:, V, s], mv[:, s, :, 1], EPS, None, ALU.add).then_inc(v_set, 1)

            def normalise(s):
                dve.wait_ge(root_set, s + 1)
                nc.vector.reciprocal(ln[:, R0, s], ln[:, ROOT, s]).then_inc(r0_set, 1)
                dve.wait_ge(r0_set, s + 1)
                k = 3 * s
                nc.vector.tensor_tensor(ln[:, SQ, s], ln[:, R0, s], ln[:, R0, s], ALU.mult).then_inc(rstd_step, 1)
                dve.wait_ge(rstd_step, k + 1)
                nc.vector.scalar_tensor_tensor(out=ln[:, VSQ, s], in0=ln[:, SQ, s], scalar=-0.5, in1=ln[:, V, s],
                                               op0=ALU.mult, op1=ALU.mult).then_inc(rstd_step, 1)
                dve.wait_ge(rstd_step, k + 2)
                nc.vector.scalar_tensor_tensor(out=ln[:, RSTD, s], in0=ln[:, VSQ, s], scalar=1.5, in1=ln[:, R0, s],
                                               op0=ALU.add, op1=ALU.mult).then_inc(rstd_step, 1)
                dve.wait_ge(rstd_step, k + 3)
                for t in range(TILES):
                    nc.vector.tensor_scalar(xn[:, s, t], x_sb[:, s, t], mv[:, s, t, 0:1], ln[:, RSTD, s, t:t + 1],
                                            ALU.subtract, ALU.mult).then_inc(xn_set, 1)

            def xt_lo_of(s):
                for c in range(KC):
                    dve.wait_ge(xt_hi_set, KC * s + c + 1)
                    nc.vector.tensor_tensor(xt_lo[:, s, c], slot[T_SLOT[s]][:, c], xt_hi[:, s, c].bitcast(f32), ALU.subtract).then_inc(xt_lo_set, 1)

            for i in range(2):
                dve.wait_ge(x_loaded[i], 16)
                statistics(0, range(i * TILES // 2, (i + 1) * TILES // 2))
            variance(0)
            normalise(0)
            dve.wait_ge(x_loaded[2], 16)
            statistics(1, range(TILES))
            variance(1)
            normalise(1)
            xt_lo_of(0)
            dve.wait_ge(par_loaded, 16)
            nc.vector.tensor_scalar(half_b[:, :], par[:, B_IG:B_IG + 2 * KC], 0.5, None, ALU.mult).then_inc(half_b_set, 1)
            dve.wait_ge(sum13_psum, 1)
            nc.vector.tensor_scalar(thr[:, 0], sums13, 0.5 / WEIGHTS, None, ALU.mult).then_inc(thr_set, 1)
            nc.vector.tensor_scalar(thr[:, 1], sums13, -0.5 / WEIGHTS, None, ALU.mult).then_inc(thr_set, 1)
            nc.vector.tensor_scalar(scale[:, 0:2], sums13, 1.0 / WEIGHTS, None, ALU.mult).then_inc(thr_set, 1)
            dve.wait_ge(thr_set, 2)
            dve.wait_ge(gaps_set, 1)
            xt_lo_of(1)
            parts = (slice(0, W3_AT), slice(W3_AT, W13))
            for i, cols in enumerate(parts):
                nc.vector.tensor_scalar(below[:, :, cols], w13_raw[:, :, cols], thr[:, 1, i:i + 1], None, ALU.is_lt).then_inc(below_set, 1)
            for i, cols in enumerate(parts):
                dve.wait_ge(below_set, i + 1)
                nc.vector.scalar_tensor_tensor(out=w13_q[:, :, cols], in0=w13_raw[:, :, cols], scalar=thr[:, 0, i:i + 1],
                                               in1=below[:, :, cols], op0=ALU.is_gt, op1=ALU.subtract).then_inc(w13_q_set, 1)
            dve.wait_ge(sum2_psum, 1)
            nc.vector.tensor_scalar(scale[:, 2:3], sum2, 1.0 / WEIGHTS, None, ALU.mult).then_inc(s2_ready, 1)
            nc.vector.tensor_scalar(thr2[:, 0:1], sum2, 0.5 / WEIGHTS, None, ALU.mult).then_inc(s2_ready, 1)
            nc.vector.tensor_scalar(thr2[:, 1:2], sum2, -0.5 / WEIGHTS, None, ALU.mult).then_inc(s2_ready, 1)
            dve.wait_ge(s2_ready, 1)
            dve.wait_ge(thr_set, 3)
            nc.vector.tensor_tensor(s32[:, :], scale[:, 1:2], scale[:, 2:3], ALU.mult).then_inc(scale2_set, 1)

            def convolve(s):
                for i in range(1, TAPS):
                    k = TAPS - 1 - i
                    for c in range(KC):
                        if i == 1:
                            dve.wait_ge(tap_set, KC * s + c + 1)
                        else:
                            dve.wait_ge(tap_step, KC * (TAPS - 2) * s + KC * (i - 2) + c + 1)
                        nc.vector.scalar_tensor_tensor(
                            out=conv[:, s, c], in0=xb[:, s, c, k:k + SEQ],
                            scalar=par[:, CONV_W + KC * k + c:CONV_W + KC * k + c + 1],
                            in1=conv[:, s, c], op0=ALU.mult, op1=ALU.add).then_inc(conv_set if i == TAPS - 1 else tap_step, 1)
                dve.wait_ge(conv_set, KC * (s + 1))
                nc.vector.memset(xb[:, s, :, TAPS - 1:TAPS], 0.5).then_inc(mult0_set, 1)

            def ternary_w2():
                dve.wait_ge(s2_ready, 3)
                dve.wait_ge(w13_q_set, 2)
                b2 = below[:, :, :].rearrange("p c n -> p (c n)")[:, 0:(FULL + 1) * D].rearrange("p (j d) -> p j d", d=D)
                nc.vector.tensor_scalar(b2, w2_raw[:, :, :], thr2[:, 1:2], None, ALU.is_lt).then_inc(below_set, 1)
                dve.wait_ge(below_set, 3)
                nc.vector.scalar_tensor_tensor(out=w2_q[:, :, :], in0=w2_raw[:, :, :], scalar=thr2[:, 0:1], in1=b2,
                                               op0=ALU.is_gt, op1=ALU.subtract).then_inc(w2_q_set, 1)

            def g_of(n):
                s, j = HJ[n]
                if n == 0:
                    dve.wait_ge(scale2_set, 1)
                dve.wait_ge(silu_set, n + 1)
                if n >= RING:
                    dve.wait_ge(g_lo_set, n - RING + 1)
                nc.vector.scalar_tensor_tensor(out=g[:, n % RING], in0=silu[:, n % RING], scalar=s32[:, 0:1],
                                               in1=slot[H_SLOT[s][j]][:, 1], op0=ALU.mult, op1=ALU.mult).then_inc(g_set, 1)

            def gated_input(s):
                dve.wait_ge(tx_set, KC * (s + 1))
                nc.vector.scalar_tensor_tensor(out=tx[:, s], in0=tx[:, s], scalar=1.0, in1=conv[:, s],
                                               op0=ALU.add, op1=ALU.mult).then_inc(nx_step, 1)

            def squares(s):
                dve.wait_ge(a_set, KC * (s + 1))
                nc.vector.tensor_tensor(xb[:, s, :, TAPS:], ta[:, s, :, 1:], ta[:, s, :, 1:], ALU.mult).then_inc(a2_set, 1)

            def recurrence(s):
                dve.wait_ge(mult_set, s + 1)
                dve.wait_ge(mult0_set, s + 1)
                dve.wait_ge(nx_step, s + 1)
                nc.vector.tensor_tensor(tx[:, s], tx[:, s], xb[:, s, :, TAPS - 1:], ALU.mult).then_inc(nx_set, 1)
                dve.wait_ge(nx_set, s + 1)
                for c in range(KC):
                    nc.vector.tensor_tensor_scan(tx[:, s, c], ta[:, s, c], tx[:, s, c], 0.0, ALU.mult, ALU.add).then_inc(h_set, 1)

            def gate_output(s):
                dve.wait_ge(h_set, KC * (s + 1))
                dve.wait_ge(y_set, KC * (s + 1))
                nc.vector.tensor_tensor(tx[:, s], tx[:, s], y[:, s], ALU.mult).then_inc(hy_set, 1)

            def lo_of_hy(s):
                dve.wait_ge(hy_hi_set, s + 1)
                nc.vector.tensor_tensor(conv_lo[:, s], tx[:, s], conv_hi[:, s].bitcast(f32), ALU.subtract).then_inc(hy_lo_set, 1)

            def output(s):
                for i in range(2):
                    dve.wait_ge(o_psum, 2 * s + i + 1)
                    dve.wait_ge(x_res_set, TILES * (s + 1))
                    t = slice(i * TILES // 2, (i + 1) * TILES // 2)
                    nc.vector.tensor_tensor(x_sb[:, s, t], slot[O_SLOT[s]][:, i].rearrange("p (t d) -> p t d", d=D), x_sb[:, s, t], ALU.add).then_inc(o_set, 1)

            convolve(0)
            convolve(1)
            g_of(0)
            g_of(1)
            dve.wait_ge(sp_log, 1)
            nc.vector.scalar_tensor_tensor(out=sp_e[:, 1], in0=par[:, A_PARAM:A_PARAM + KC], scalar=0.0, in1=sp_e[:, 2],
                                           op0=ALU.max, op1=ALU.add).then_inc(rate_set, 1)
            dve.wait_ge(rate_set, 1)
            nc.vector.tensor_scalar(a_rate[:, :], sp_e[:, 1], -4.0, None, ALU.mult).then_inc(rate_set, 1)
            g_of(2)
            ternary_w2()
            gated_input(0)
            g_of(3)
            g_of(4)
            dve.wait_ge(silu_t_set, 1)
            nc.vector.scalar_tensor_tensor(out=g_t[HALF:HALF + TAIL], in0=silu_t[HALF:HALF + TAIL], scalar=s32[HALF:HALF + TAIL, 0:1],
                                           in1=slot[TAIL_SLOT][HALF:HALF + TAIL].rearrange("p s n -> p (s n)"), op0=ALU.mult, op1=ALU.mult).then_inc(g_t_set, 1)
            dve.wait_ge(g_t_set, 1)
            dve.wait_ge(pads_set, 2)
            nc.vector.tensor_copy(gt_hi[HALF:HALF + TAIL].rearrange("p s n -> p (s n)"), g_t[HALF:HALF + TAIL]).then_inc(gt_hi_set, 1)
            nc.vector.tensor_copy(gt[0:TAIL].rearrange("p s n -> p (s n)"), g_t[HALF:HALF + TAIL]).then_inc(gt_hi_set, 1)
            dve.wait_ge(gt_hi_set, 1)
            nc.vector.tensor_tensor(gt[HALF:HALF + TAIL].rearrange("p s n -> p (s n)"), g_t[HALF:HALF + TAIL],
                                    gt_hi[HALF:HALF + TAIL].rearrange("p s n -> p (s n)").bitcast(f32), ALU.subtract).then_inc(gt_lo_set, 1)
            gated_input(1)
            g_of(5)
            g_of(6)
            squares(0)
            squares(1)
            recurrence(0)
            g_of(7)
            gate_output(0)
            g_of(8)
            g_of(9)
            recurrence(1)
            lo_of_hy(0)
            gate_output(1)
            lo_of_hy(1)
            output(0)
            output(1)

        @block.tensor
        def _(pe):
            def transposes(s):
                for c in range(KC):
                    for t in range(TILES):
                        if c == 0:
                            pe.wait_ge(xn_set, TILES * s + t + 1)
                        mm = nc.tensor.transpose(slot[T_SLOT[s]][:, c, t * P:(t + 1) * P], xn[:, s, t, c * P:(c + 1) * P], ident[:, :])
                    mm.then_inc(xt_psum, 1)

            def dense_terms(dst, m, terms, first, last, chunk_ready=None):
                for c in range(KC):
                    if chunk_ready:
                        pe.wait_ge(chunk_ready[0], chunk_ready[1] + c)
                    for o in range(KC):
                        for i, (w, v) in enumerate(terms):
                            mm = nc.tensor.matmul(dst[:, o], w[:, m, c, o * P:(o + 1) * P], v[:, c], start=(first and i == 0 and c == 0),
                                                  stop=(last and i == len(terms) - 1 and c == KC - 1))
                return mm

            def dense_product(dst, m, hi, lo, done, hi_ready=None, lo_ready=None, between=None):
                dense_terms(dst, m, [(w_hi, hi), (w_lo, hi)], True, False, hi_ready)
                if between:
                    between()
                dense_terms(dst, m, [(w_hi, lo)], False, True, lo_ready).then_inc(done, 1)

            def hidden(n):
                s, j = HJ[n]
                for o, col in enumerate((j * P, W3_AT + TAIL + j * P)):
                    for c in range(KC):
                        for v in (xt_hi, xt_lo):
                            mm = nc.tensor.matmul(slot[H_SLOT[s][j]][:, o], w13_q[:, c, col:col + P], v[:, s, c],
                                                  start=(c == 0 and v is xt_hi), stop=(c == KC - 1 and v is xt_lo))
                mm.then_inc(h_psum, 1)

            def hidden_tail():
                for s in range(SEQS):
                    for c in range(KC):
                        for v in (xt_hi, xt_lo):
                            mm = nc.tensor.matmul(slot[TAIL_SLOT][:, s], w13_q[:, c, FULL * P:(FULL + 1) * P], v[:, s, c],
                                                  start=(c == 0 and v is xt_hi), stop=(c == KC - 1 and v is xt_lo))
                mm.then_inc(t_psum, 1)

            def out_tile(s, t):
                return slot[O_SLOT[s]][:, t // 2, (t % 2) * D:(t % 2 + 1) * D]

            def down(s):
                for j in range(FULL + 1):
                    if j < FULL:
                        pe.wait_ge(g_lo_set, FULL * s + j + 1)
                    else:
                        pe.wait_ge(gt_lo_set, 1)
                    for t in range(TILES):
                        rows = slice(t * P, (t + 1) * P)
                        if j < FULL:
                            for v in (g_hi, g_lo):
                                nc.tensor.matmul(out_tile(s, t), v[:, j, s, rows], w2_q[:, j], start=(j == 0 and t % 2 == 0 and v is g_hi),
                                                 stop=False, skip_group_check=True)
                        else:
                            nc.tensor.matmul(out_tile(s, t), gt[:, s, rows], w2_q[:, j], start=False, stop=False, skip_group_check=True)

            def project(s):
                pe.wait_ge(w_lo_set, WOUT + 1)
                pe.wait_ge(hy_lo_set, s + 1)
                for t in range(TILES):
                    rows = slice(t * P, (t + 1) * P)
                    terms = [(conv_hi, w_hi), (conv_lo, w_hi), (conv_hi, w_lo)]
                    for i, (v, w) in enumerate(terms):
                        for c in range(KC):
                            mm = nc.tensor.matmul(out_tile(s, t), v[:, s, c, rows], w[:, WOUT, c], start=False,
                                                  stop=(i == len(terms) - 1 and c == KC - 1), skip_group_check=True)
                    if t % 2:
                        mm.then_inc(o_psum, 1)

            pe.wait_ge(ident_set, 1)
            transposes(0)
            def second_transposes_and_sums():
                transposes(1)
                pe.wait_ge(consts_set, 3)
                pe.wait_ge(abs13_set, 2)
                nc.tensor.matmul(sums13, ones[:, :], abs_sum[:, 0:2], start=True, stop=True).then_inc(sum13_psum, 1)

            pe.wait_ge(w_lo_set, WX + 1)
            dense_product(slot[X_SLOT[0]], WX, xt_hi[:, 0], xt_lo[:, 0], xb_psum, (xt_hi_set, 1), (xt_lo_set, 1),
                          between=second_transposes_and_sums)
            pe.wait_ge(thr_set, 3)
            dense_product(slot[X_SLOT[1]], WX, xt_hi[:, 1], xt_lo[:, 1], xb_psum, (xt_hi_set, KC + 1), (xt_lo_set, KC + 1))
            pe.wait_ge(w_lo_set, WY + 1)
            dense_product(slot[Y_SLOT[0]], WY, xt_hi[:, 0], xt_lo[:, 0], y_psum)
            pe.wait_ge(abs2_set, 2)
            pe.wait_ge(xb_set, KC)
            for i in range(2):
                mm = nc.tensor.matmul(sum2, ones[:, :], abs_sum[:, 2 + i:3 + i], start=(i == 0), stop=(i == 1))
            mm.then_inc(sum2_psum, 1)
            dense_product(slot[Y_SLOT[1]], WY, xt_hi[:, 1], xt_lo[:, 1], y_psum)
            pe.wait_ge(w13_q_set, 2)
            pe.wait_ge(s2_ready, 3)
            hidden(0)
            pe.wait_ge(xb_set, 2 * KC)
            hidden(1)
            pe.wait_ge(y_set, KC)
            hidden(2)
            pe.wait_ge(w_lo_set, WAG + 1)

            def gate_products(s):
                if s == 0:
                    pe.wait_ge(y_set, 2 * KC)
                else:
                    pe.wait_ge(ta_set, KC)
                dense_product(slot[GX_SLOT[s]], WIG, conv_hi[:, s], conv_lo[:, s], gx_psum,
                              (conv_hi_set, KC * s + 1), (conv_lo_set, KC * s + 1))
                pe.wait_ge(g_set, 1 if s == 0 else 4)
                dense_product(slot[GA_SLOT[s]], WAG, conv_hi[:, s], conv_lo[:, s], ga_psum)

            gate_products(0)
            pe.wait_ge(g_set, 2)
            hidden(3)
            pe.wait_ge(g_set, 3)
            hidden(4)
            pe.wait_ge(tx_set, KC)
            hidden_tail()
            gate_products(1)
            pe.wait_ge(g_t_set, 1)
            hidden(5)
            pe.wait_ge(g_set, 5)
            hidden(6)
            pe.wait_ge(tx_set, 2 * KC)
            pe.wait_ge(w2_q_set, 1)
            down(0)
            pe.wait_ge(ta_set, 2 * KC)
            hidden(7)
            pe.wait_ge(g_set, 6)
            hidden(8)
            pe.wait_ge(g_set, 7)
            hidden(9)
            pe.wait_ge(g_set, 8)
            down(1)
            project(0)
            project(1)


def kernel(L0_attn_x, L0_attn_w_y, L0_attn_b_y, L0_attn_w_x, L0_attn_b_x, L0_attn_conv_w, L0_attn_conv_b,
           L0_attn_a_param, L0_attn_w_ig, L0_attn_b_ig, L0_attn_w_ag, L0_attn_b_ag, L0_attn_w_out, L0_attn_b_out,
           L0_ffn_w1, L0_ffn_w3, L0_ffn_w2):
    import numpy as np
    import concourse.bacc as bacc
    from concourse.bass_utils import run_bass_kernel_spmd

    x = np.ascontiguousarray(L0_attn_x)
    w3t = np.asarray(L0_ffn_w3).T
    vectors = [L0_attn_b_y, L0_attn_b_x, L0_attn_conv_b, L0_attn_a_param, L0_attn_b_ig, L0_attn_b_ag, *L0_attn_conv_w]
    arrays = {
        "x": x.reshape(TOKENS, D),
        "dense": np.stack([L0_attn_w_x, L0_attn_w_y, L0_attn_w_ig, L0_attn_w_ag, L0_attn_w_out]),
        "w13t": np.concatenate([np.asarray(L0_ffn_w1).T, w3t[:, FULL * P:], w3t[:, :FULL * P]], axis=1),
        "w2t": np.asarray(L0_ffn_w2).T,
        "params": np.stack(vectors).reshape(len(vectors) * KC, P).T,
        "b_out": np.asarray(L0_attn_b_out),
    }
    arrays = {k: np.ascontiguousarray(v) for k, v in arrays.items()}
    nc = bacc.Bacc("TRN2", target_bir_lowering=False, num_devices=1)
    aps = [nc.dram_tensor(k, v.shape, mybir.dt.from_np(v.dtype), kind="ExternalInput").ap() for k, v in arrays.items()]
    out = nc.dram_tensor("out", (TOKENS, D), mybir.dt.float32, kind="ExternalOutput").ap()
    build(nc, *aps, out)
    result = run_bass_kernel_spmd(nc, [arrays], core_ids=[0])
    return result.results[0]["out"].reshape(x.shape)
```

```python
from contextlib import ExitStack

import concourse.bass as bass
from concourse import mybir

P = 128
SEQS, SEQ = 2, 512
TOKENS = SEQS * SEQ
D = 256
HIDDEN = 682
TAPS = 4
KC = D // P
TILES = SEQ // P
FULL = HIDDEN // P
TAIL = HIDDEN - FULL * P
HALF = 64
W3_AT = FULL * P + HALF
W13 = W3_AT + HIDDEN
EPS = 1e-5
WARM = 12
WEIGHTS = D * HIDDEN

B_Y, B_X, CONV_B, A_PARAM, B_IG, B_AG, CONV_W = (KC * i for i in range(7))
PARAMS = CONV_W + KC * TAPS
WX, WY, WIG, WAG, WOUT = range(5)


def build(nc: bass.Bass, x, dense, w13t, w2t, params, b_out, out):
    f32, f32r, bf16 = mybir.dt.float32, mybir.dt.float32r, mybir.dt.bfloat16
    ALU, ACT = mybir.AluOpType, mybir.ActivationFunctionType

    x_dram = x.rearrange("(s t p) d -> s p t d", s=SEQS, p=P)
    out_dram = out.rearrange("(s t p) d -> s p t d", s=SEQS, p=P)

    ctx = ExitStack()
    with ctx:
        def sb(name, shape, dt=f32):
            return ctx.enter_context(nc.sbuf_tensor(name, shape, dt))

        def sem(name):
            return ctx.enter_context(nc.semaphore(name))

        x_sb = sb("x_sb", [P, SEQS, TILES, D])
        xn_y = sb("xn_y", [P, SEQS * TILES * D])
        xn = xn_y[:, :].rearrange("p (s t d) -> p s t d", s=SEQS, t=TILES)
        y = xn_y[:, :].rearrange("p (s c n) -> p s c n", s=SEQS, c=KC)
        xt_hi = sb("xt_hi", [P, SEQS, KC, SEQ], f32r)
        xt_lo = sb("xt_lo", [P, SEQS, KC, SEQ], f32r)
        w_raw = sb("w_raw", [P, 5, KC, D])
        w_hi = sb("w_hi", [P, 5, KC, D], f32r)
        w_lo = sb("w_lo", [P, 5, KC, D], f32r)
        w13_raw = sb("w13_raw", [P, KC, W13])
        w13_q = sb("w13_q", [P, KC, W13], f32r)
        below = sb("below", [P, KC, W13], bf16)
        w2_raw = sb("w2_raw", [P, FULL + 1, D])
        w2_q = sb("w2_q", [P, FULL + 1, D], f32r)
        xb = sb("xb", [P, SEQS, KC, TAPS - 1 + SEQ])
        conv = sb("conv", [P, SEQS, KC, SEQ])
        conv_hi = sb("conv_hi", [P, SEQS, KC, SEQ], f32r)
        conv_lo = sb("conv_lo", [P, SEQS, KC, SEQ], f32r)
        tx = sb("tx", [P, SEQS, KC, SEQ])
        ta = sb("ta", [P, SEQS, KC, SEQ])
        g_hi = sb("g_hi", [P, FULL, SEQS, SEQ], f32r)
        g_lo = sb("g_lo", [P, FULL, SEQS, SEQ], f32r)
        gt = sb("gt", [P, SEQS, SEQ], f32r)
        gt_hi = sb("gt_hi", [P, SEQS, SEQ], f32r)
        RING = 3
        par = sb("par", [P, PARAMS])
        half_b = sb("half_b", [P, 2 * KC])
        a_rate = sb("a_rate", [P, KC])
        sp_e = sb("sp_e", [P, 3, KC])
        b_out_bc = sb("b_out_bc", [P, D])
        ident = sb("ident", [P, P])
        ones = sb("ones", [P, P])
        stats = sb("stats", [P, SEQS, TILES, 6])
        mv = sb("mv", [P, SEQS, TILES, 2])
        ln = sb("ln", [P, 6, SEQS, TILES])
        V, ROOT, R0, SQ, VSQ, RSTD = range(6)
        abs_sum = sb("abs_sum", [P, 4])
        thr = sb("thr", [P, 2, 2])
        scale = sb("scale", [P, 3])
        thr2 = sb("thr2", [P, 2])
        eps = sb("eps", [P, 1])
        quarter = sb("quarter", [P, 1])
        s32 = sb("s32", [P, 1])

        w_flat = w_raw[:, :, :, :].rearrange("p m c n -> p (m c n)")
        silu = w_flat[:, 0:RING * SEQ].rearrange("p (r n) -> p r n", r=RING)
        silu_t = w_flat[:, RING * SEQ:RING * SEQ + TOKENS]
        w13_flat = w13_raw[:, :, :].rearrange("p c n -> p (c n)")
        g = w13_flat[:, 0:RING * SEQ].rearrange("p (r n) -> p r n", r=RING)
        g_t = w13_flat[:, RING * SEQ:RING * SEQ + TOKENS]

        slot = [ctx.enter_context(nc.psum_tensor(f"slot{i}", [P, 2, SEQ], f32)) for i in range(4)]
        T_SLOT, X_SLOT, Y_SLOT = (0, 1), (2, 0), (3, 1)
        H_SLOT = ((2, 3, 0, 1, 2), (3, 0, 0, 1, 2))
        TAIL_SLOT = 3
        GX_SLOT, GA_SLOT = (1, 3), (2, 0)
        O_TILES = ((range(0, 2), range(2, 4)), (range(0, 2), range(2, 3), range(3, 4)))
        O_BANK = ((slot[1][:, 0], slot[1][:, 1]), (slot[2][:, 0], slot[2][:, 1], slot[3][:, 0]))
        O_ALL = [(s, i) for s in range(SEQS) for i in range(len(O_TILES[s]))]
        sums13 = slot[0][:, 0, 0:2]
        sum2 = slot[2][:, 0, 0:2]
        WARM_SLOT = 3

        halves = (slice(0, SEQ // 2), slice(SEQ // 2, SEQ))

        def xt_bank(s, h):
            return slot[T_SLOT[s]][:, h].rearrange("p (c n) -> p c n", c=KC)

        x_loaded = [sem(f"x_loaded{i}") for i in range(3)]
        w_loaded = [sem(f"w_loaded{m}") for m in range(5)]
        w1_loaded, w3_loaded = sem("w1_loaded"), sem("w3_loaded")
        w2_loaded = sem("w2_loaded")
        par_loaded, b_out_loaded = sem("par_loaded"), sem("b_out_loaded")
        out_stored = sem("out_stored")
        ones_set = sem("ones_set")
        consts_set, ident_set, pads_set = sem("consts_set"), sem("ident_set"), sem("pads_set")
        eps_set = sem("eps_set")
        quarter_set = sem("quarter_set")
        gaps_set = sem("gaps_set")
        stats_set, mv_set, v_set = sem("stats_set"), sem("mv_set"), sem("v_set")
        root_set, r0_set, rstd_step = sem("root_set"), sem("r0_set"), sem("rstd_step")
        xn_set, xt_psum, xt_hi_set, xt_lo_set = sem("xn_set"), sem("xt_psum"), sem("xt_hi_set"), sem("xt_lo_set")
        w_hi_set = sem("w_hi_set")
        w_lo_set = sem("w_lo_set")
        sp_abs, sp_exp, sp_log, rate_set, half_b_set = (
            sem("sp_abs"), sem("sp_exp"), sem("sp_log"), sem("rate_set"), sem("half_b_set"))
        abs13_set, abs2_set, sum13_psum, sum2_psum = (
            sem("abs13_set"), sem("abs2_set"), sem("sum13_psum"), sem("sum2_psum"))
        thr_set, scale2_set, s2_ready = sem("thr_set"), sem("scale2_set"), sem("s2_ready")
        below_set, w13_q_set, w2_q_set = sem("below_set"), sem("w13_q_set"), sem("w2_q_set")
        xb_psum, xb_set = sem("xb_psum"), sem("xb_set")
        tap_set, tap_step, conv_set = sem("tap_set"), sem("tap_step"), sem("conv_set")
        conv_hi_set, conv_lo_set = sem("conv_hi_set"), sem("conv_lo_set")
        y_psum, y_set = sem("y_psum"), sem("y_set")
        gx_psum, ga_psum, tx_set, ta_set = sem("gx_psum"), sem("ga_psum"), sem("tx_set"), sem("ta_set")
        a_set, a2_set, mult_set, mult0_set = sem("a_set"), sem("a2_set"), sem("mult_set"), sem("mult0_set")
        nx_last_set = sem("nx_last_set")
        nx_step, nx_set, h_set, hy_set = sem("nx_step"), sem("nx_set"), sem("h_set"), sem("hy_set")
        hy_hi_set, hy_lo_set = sem("hy_hi_set"), sem("hy_lo_set")
        h_psum, silu_set, g_set, g_hi_set, g_lo_set = (
            sem("h_psum"), sem("silu_set"), sem("g_set"), sem("g_hi_set"), sem("g_lo_set"))
        t_psum, silu_t_set, g_t_set, gt_hi_set, gt_lo_set = (
            sem("t_psum"), sem("silu_t_set"), sem("g_t_set"), sem("gt_hi_set"), sem("gt_lo_set"))
        x_res_set, o_psum, o_set = sem("x_res_set"), sem("o_psum"), sem("o_set")

        LAST_HI = 2 * FULL - 2
        HJ = [(s, j) for s in range(SEQS) for j in range(FULL)]

        block = ctx.enter_context(nc.Block())

        @block.sync
        def _(sp):
            def square(m):
                sp.dma_start(w_raw[:, m], dense[m].rearrange("(c p) n -> p c n", p=P)).then_inc(w_loaded[m], 16)

            for i in range(2):
                t = slice(i * TILES // 2, (i + 1) * TILES // 2)
                sp.dma_start(x_sb[:, 0, t], x_dram[0][:, t]).then_inc(x_loaded[i], 16)
            square(WX)
            sp.dma_start(x_sb[:, 1], x_dram[1]).then_inc(x_loaded[2], 16)
            square(WY)
            w13_dram = w13t.rearrange("(c p) n -> p c n", p=P)
            sp.dma_start(w13_raw[:, :, 0:HIDDEN], w13_dram[:, :, 0:HIDDEN]).then_inc(w1_loaded, 16)
            sp.dma_start(w13_raw[:, :, W3_AT:W13], w13_dram[:, :, HIDDEN:2 * HIDDEN]).then_inc(w3_loaded, 16)
            sp.dma_start(w2_raw[:, 0:FULL], w2t[0:FULL * P].rearrange("(j p) n -> p j n", p=P)).then_inc(w2_loaded, 16)
            sp.wait_ge(gaps_set, 2)
            sp.dma_start(w2_raw[0:TAIL, FULL], w2t[FULL * P:HIDDEN]).then_inc(w2_loaded, 16)
            sp.dma_start(w2_raw[HALF:HALF + TAIL, FULL], w2t[FULL * P:HIDDEN]).then_inc(w2_loaded, 16)
            square(WIG)
            square(WAG)
            square(WOUT)
            sp.dma_start(b_out_bc[:, :], b_out.partition_broadcast(P)).then_inc(b_out_loaded, 16)
            for n, (s, i) in enumerate(O_ALL):
                sp.wait_ge(o_set, n + 1)
                t = slice(O_TILES[s][i].start, O_TILES[s][i].stop)
                sp.dma_start(out_dram[s][:, t], x_sb[:, s, t]).then_inc(out_stored, 16)
            sp.wait_ge(out_stored, 16 * len(O_ALL))

        @block.gpsimd
        def _(pool):
            nc.gpsimd.memset(ones[:, :], 1.0).then_inc(ones_set, 1)
            nc.gpsimd.memset(ident[:, :], 0.0).then_inc(consts_set, 1)
            nc.gpsimd.memset(w13_raw[:, :, HIDDEN:W3_AT], 0.0).then_inc(gaps_set, 1)
            nc.gpsimd.memset(w2_raw[:, FULL, :], 0.0).then_inc(gaps_set, 1)
            pool.wait_ge(consts_set, 1)
            nc.gpsimd.affine_select(out=ident[:, :], in_=ident[:, :], compare_op=ALU.not_equal, fill=1.0, base=0,
                                    pattern=[[-1, P]], channel_multiplier=1).then_inc(ident_set, 1)
            nc.gpsimd.memset(abs_sum[:, 3:4], 0.0).then_inc(consts_set, 1)
            nc.gpsimd.memset(xb[:, :, :, 0:TAPS - 1], 0.0).then_inc(pads_set, 1)
            nc.gpsimd.memset(gt[:, :, :].bitcast(f32), 0.0).then_inc(pads_set, 1)

            def square_lo(m):
                pool.wait_ge(w_hi_set, m + 1)
                nc.gpsimd.tensor_tensor(w_lo[:, m], w_raw[:, m], w_hi[:, m].bitcast(f32), ALU.subtract).then_inc(w_lo_set, 1)

            def newest_tap(s):
                for c in range(KC):
                    pool.wait_ge(xb_set, KC * s + c + 1)
                    k = TAPS - 1
                    nc.gpsimd.tensor_scalar(conv[:, s, c], xb[:, s, c, k:k + SEQ],
                                            par[:, CONV_W + KC * k + c:CONV_W + KC * k + c + 1],
                                            par[:, CONV_B + c:CONV_B + c + 1], ALU.mult, ALU.add).then_inc(tap_set, 1)

            def residual(s):
                pool.wait_ge(xn_set, TILES * (s + 1))
                pool.wait_ge(b_out_loaded, 16)
                for t in range(TILES):
                    nc.gpsimd.tensor_tensor(x_sb[:, s, t], x_sb[:, s, t], b_out_bc[:, :], ALU.add).then_inc(x_res_set, 1)

            def lo_of_conv(s):
                for c in range(KC):
                    pool.wait_ge(conv_hi_set, KC * s + c + 1)
                    nc.gpsimd.tensor_tensor(conv_lo[:, s, c], conv[:, s, c], conv_hi[:, s, c].bitcast(f32), ALU.subtract).then_inc(conv_lo_set, 1)

            def lo_of_g(n):
                s, j = HJ[n]
                pool.wait_ge(g_hi_set, n + 1)
                nc.gpsimd.tensor_tensor(g_lo[:, j, s], g[:, n % RING], g_hi[:, j, s].bitcast(f32), ALU.subtract).then_inc(g_lo_set, 1)

            square_lo(WX)
            square_lo(WY)
            pool.wait_ge(par_loaded, 16)
            newest_tap(0)
            newest_tap(1)
            square_lo(WIG)
            square_lo(WAG)
            lo_of_conv(0)
            square_lo(WOUT)
            for n in range(6):
                lo_of_g(n)
            lo_of_conv(1)
            for n in range(6, 2 * FULL):
                lo_of_g(n)
            residual(0)
            residual(1)
            for s in range(SEQS):
                pool.wait_ge(mult0_set, s + 1)
                pool.wait_ge(nx_step, s + 1)
                pool.wait_ge(mult_set, KC * (s + 1))
                nc.gpsimd.tensor_tensor(tx[:, s, 1], tx[:, s, 1], xb[:, s, 1, TAPS - 1:], ALU.mult).then_inc(nx_last_set, 1)
            for c in range(KC):
                pool.wait_ge(hy_hi_set, c + 1)
                nc.gpsimd.tensor_tensor(conv_lo[:, 0, c], tx[:, 0, c], conv_hi[:, 0, c].bitcast(f32), ALU.subtract).then_inc(hy_lo_set, 1)

        @block.scalar
        def _(act):
            act.dma_start(par[:, :], params).then_inc(par_loaded, 16)

            def square_hi(m):
                act.wait_ge(w_loaded[m], 16)
                nc.scalar.activation(w_hi[:, m], w_raw[:, m], ACT.Copy).then_inc(w_hi_set, 1)

            def root_of(s):
                act.wait_ge(mv_set, TILES * (s + 1))
                act.wait_ge(eps_set, 1)
                nc.scalar.activation(ln[:, ROOT, s], mv[:, s, :, 1], ACT.Sqrt, bias=eps[:, 0:1]).then_inc(root_set, 1)

            def xt_hi_of(s):
                for h in range(2):
                    act.wait_ge(xt_psum, 2 * s + h + 1)
                    nc.scalar.activation(xt_hi[:, s, :, halves[h]], xt_bank(s, h), ACT.Copy).then_inc(xt_hi_set, 1)

            junk_a = tx[:, :, :, :].rearrange("p s c n -> p (s c n)")
            junk_b = ta[:, :, :, :].rearrange("p s c n -> p (s c n)")
            junk_c = g_hi[:, :, :, :].rearrange("p j s n -> p (j s n)")

            def abs_sum_of(src, chunks, junk, col, done):
                parts, n = src.shape[0], src.shape[-1]
                out = junk[0:parts, 0:chunks * n]
                if chunks > 1:
                    out = out.rearrange("p (c n) -> p c n", c=chunks)
                nc.scalar.activation(out, src, ACT.Abs, accum_out=abs_sum[0:parts, col:col + 1]).then_inc(done, 1)

            act.wait_ge(par_loaded, 16)
            a_par = par[:, A_PARAM:A_PARAM + KC]
            nc.scalar.activation(sp_e[:, 0], a_par, ACT.Abs).then_inc(sp_abs, 1)
            act.wait_ge(sp_abs, 1)
            nc.scalar.activation(sp_e[:, 1], sp_e[:, 0], ACT.Exp, scale=-1.0).then_inc(sp_exp, 1)
            root_of(0)
            square_hi(WX)
            square_hi(WY)
            xt_hi_of(0)
            root_of(1)
            act.wait_ge(w1_loaded, 16)
            abs_sum_of(w13_raw[:, :, 0:HIDDEN], KC, junk_a, 0, abs13_set)
            act.wait_ge(w3_loaded, 16)
            abs_sum_of(w13_raw[:, :, W3_AT:W13], KC, junk_b, 1, abs13_set)
            act.wait_ge(sp_exp, 1)
            nc.scalar.activation(sp_e[:, 2], sp_e[:, 1], ACT.Ln, bias=1.0).then_inc(sp_log, 1)
            xt_hi_of(1)

            def xb_of(s):
                act.wait_ge(pads_set, 1)
                act.wait_ge(xb_psum, s + 1)
                for c in range(KC):
                    nc.scalar.activation(xb[:, s, c, TAPS - 1:], slot[X_SLOT[s]][:, c], ACT.Identity,
                                         bias=par[:, B_X + c:B_X + c + 1]).then_inc(xb_set, 1)

            xb_of(0)
            act.wait_ge(w2_loaded, 48)
            act.wait_ge(consts_set, 2)
            abs_sum_of(w2_raw[:, 0:FULL, :], FULL, junk_c, 2, abs2_set)
            abs_sum_of(w2_raw[0:TAIL, FULL, :], 1, junk_c[:, FULL * D:], 3, abs2_set)
            xb_of(1)

            def gelu_of(s):
                act.wait_ge(y_psum, s + 1)
                for c in range(KC):
                    nc.scalar.activation(y[:, s, c], slot[Y_SLOT[s]][:, c], ACT.Gelu,
                                         bias=par[:, B_Y + c:B_Y + c + 1]).then_inc(y_set, 1)

            def silu_of(n):
                s, j = HJ[n]
                act.wait_ge(h_psum, n + 1)
                if n >= RING:
                    act.wait_ge(g_set, n - RING + 1)
                nc.scalar.activation(silu[:, n % RING], slot[H_SLOT[s][j]][:, 0], ACT.Silu,
                                     scale=scale[:, 0:1]).then_inc(silu_set, 1)

            def g_hi_of(n):
                s, j = HJ[n]
                act.wait_ge(g_set, n + 1)
                nc.scalar.activation(g_hi[:, j, s], g[:, n % RING], ACT.Copy).then_inc(g_hi_set, 1)

            def conv_hi_of(s):
                for c in range(KC):
                    act.wait_ge(conv_set, KC * s + c + 1)
                    nc.scalar.activation(conv_hi[:, s, c], conv[:, s, c], ACT.Copy).then_inc(conv_hi_set, 1)

            def gate_x(s):
                act.wait_ge(half_b_set, 1)
                act.wait_ge(gx_psum, s + 1)
                for c in range(KC):
                    nc.scalar.activation(tx[:, s, c], slot[GX_SLOT[s]][:, c], ACT.Tanh,
                                         scale=0.5, bias=half_b[:, c:c + 1]).then_inc(tx_set, 1)

            def gate_a(s):
                act.wait_ge(ga_psum, s + 1)
                for c in range(KC):
                    nc.scalar.activation(ta[:, s, c], slot[GA_SLOT[s]][:, c], ACT.Tanh,
                                         scale=0.5, bias=half_b[:, KC + c:KC + c + 1]).then_inc(ta_set, 1)

            def decays(s):
                act.wait_ge(rate_set, 2)
                for c in range(KC):
                    act.wait_ge(ta_set, KC * s + c + 1)
                    nc.scalar.activation(ta[:, s, c], ta[:, s, c], ACT.Exp, scale=a_rate[:, c:c + 1],
                                         bias=a_rate[:, c:c + 1]).then_inc(a_set, 1)

            def mult_of(s):
                act.wait_ge(quarter_set, 1)
                act.wait_ge(a2_set, s + 1)
                for c in range(KC):
                    nc.scalar.activation(xb[:, s, c, TAPS:], xb[:, s, c, TAPS:], ACT.Sqrt, scale=-0.25, bias=quarter[:, 0:1]).then_inc(mult_set, 1)

            def hy_hi_of(s, c):
                act.wait_ge(hy_set, KC * s + c + 1)
                nc.scalar.activation(conv_hi[:, s, c], tx[:, s, c], ACT.Copy).then_inc(hy_hi_set, 1)

            square_hi(WIG)
            gelu_of(0)
            gelu_of(1)
            square_hi(WAG)
            act.wait_ge(w_lo_set, WIG + 1)
            silu_of(0)
            silu_of(1)
            conv_hi_of(0)
            silu_of(2)
            g_hi_of(0)
            square_hi(WOUT)
            g_hi_of(1)
            silu_of(3)
            g_hi_of(2)
            silu_of(4)
            g_hi_of(3)
            silu_of(5)
            g_hi_of(4)
            silu_of(6)
            g_hi_of(5)
            conv_hi_of(1)
            gate_x(0)
            g_hi_of(6)
            gate_a(0)
            act.wait_ge(t_psum, 1)
            act.wait_ge(w_lo_set, WOUT + 1)
            nc.scalar.activation(silu_t[HALF:HALF + TAIL], slot[TAIL_SLOT][0:TAIL].rearrange("p s n -> p (s n)"), ACT.Silu,
                                 scale=scale[0:TAIL, 0:1]).then_inc(silu_t_set, 1)
            silu_of(7)
            silu_of(8)
            g_hi_of(7)
            silu_of(9)
            decays(0)
            gate_x(1)
            gate_a(1)
            decays(1)
            mult_of(0)
            mult_of(1)
            for s in range(SEQS):
                for c in range(KC):
                    hy_hi_of(s, c)

        @block.vector
        def _(dve):
            nc.vector.memset(eps[:, :], EPS).then_inc(eps_set, 1)
            nc.vector.memset(quarter[:, :], 0.25).then_inc(quarter_set, 1)

            def statistics(s, tiles):
                for t in tiles:
                    nc.vector.bn_stats(stats[:, s, t], x_sb[:, s, t]).then_inc(stats_set, 1)

            def variance(s):
                for t in range(TILES):
                    dve.wait_ge(stats_set, TILES * s + t + 1)
                    nc.vector.bn_aggr(mv[:, s, t], stats[:, s, t]).then_inc(mv_set, 1)
                dve.wait_ge(mv_set, TILES * (s + 1))
                nc.vector.tensor_scalar(ln[:, V, s], mv[:, s, :, 1], EPS, None, ALU.add).then_inc(v_set, 1)

            def normalise(s):
                dve.wait_ge(v_set, s + 1)
                dve.wait_ge(root_set, s + 1)
                nc.vector.reciprocal(ln[:, R0, s], ln[:, ROOT, s]).then_inc(r0_set, 1)
                dve.wait_ge(r0_set, s + 1)
                k = 3 * s
                nc.vector.tensor_tensor(ln[:, SQ, s], ln[:, R0, s], ln[:, R0, s], ALU.mult).then_inc(rstd_step, 1)
                dve.wait_ge(rstd_step, k + 1)
                nc.vector.scalar_tensor_tensor(out=ln[:, VSQ, s], in0=ln[:, SQ, s], scalar=-0.5, in1=ln[:, V, s],
                                               op0=ALU.mult, op1=ALU.mult).then_inc(rstd_step, 1)
                dve.wait_ge(rstd_step, k + 2)
                nc.vector.scalar_tensor_tensor(out=ln[:, RSTD, s], in0=ln[:, VSQ, s], scalar=1.5, in1=ln[:, R0, s],
                                               op0=ALU.add, op1=ALU.mult).then_inc(rstd_step, 1)
                dve.wait_ge(rstd_step, k + 3)
                for t in range(TILES):
                    nc.vector.tensor_scalar(xn[:, s, t], x_sb[:, s, t], mv[:, s, t, 0:1], ln[:, RSTD, s, t:t + 1],
                                            ALU.subtract, ALU.mult).then_inc(xn_set, 1)

            def xt_lo_of(s):
                for h in range(2):
                    dve.wait_ge(xt_hi_set, 2 * s + h + 1)
                    nc.vector.tensor_tensor(xt_lo[:, s, :, halves[h]], xt_bank(s, h), xt_hi[:, s, :, halves[h]].bitcast(f32), ALU.subtract).then_inc(xt_lo_set, 1)

            for i in range(2):
                dve.wait_ge(x_loaded[i], 16)
                statistics(0, range(i * TILES // 2, (i + 1) * TILES // 2))
            variance(0)
            normalise(0)
            dve.wait_ge(x_loaded[2], 16)
            statistics(1, range(TILES))
            variance(1)
            normalise(1)
            xt_lo_of(0)
            dve.wait_ge(par_loaded, 16)
            nc.vector.tensor_scalar(half_b[:, :], par[:, B_IG:B_IG + 2 * KC], 0.5, None, ALU.mult).then_inc(half_b_set, 1)
            dve.wait_ge(sum13_psum, 1)
            nc.vector.tensor_scalar(thr[:, 0], sums13, 0.5 / WEIGHTS, None, ALU.mult).then_inc(thr_set, 1)
            nc.vector.tensor_scalar(thr[:, 1], sums13, -0.5 / WEIGHTS, None, ALU.mult).then_inc(thr_set, 1)
            nc.vector.tensor_scalar(scale[:, 0:2], sums13, 1.0 / WEIGHTS, None, ALU.mult).then_inc(thr_set, 1)
            dve.wait_ge(thr_set, 2)
            dve.wait_ge(gaps_set, 1)
            parts = (slice(0, W3_AT), slice(W3_AT, W13))
            for i, cols in enumerate(parts):
                nc.vector.tensor_scalar(below[:, :, cols], w13_raw[:, :, cols], thr[:, 1, i:i + 1], None, ALU.is_lt).then_inc(below_set, 1)
            xt_lo_of(1)
            for i, cols in enumerate(parts):
                dve.wait_ge(below_set, i + 1)
                nc.vector.scalar_tensor_tensor(out=w13_q[:, :, cols], in0=w13_raw[:, :, cols], scalar=thr[:, 0, i:i + 1],
                                               in1=below[:, :, cols], op0=ALU.is_gt, op1=ALU.subtract).then_inc(w13_q_set, 1)
            dve.wait_ge(sum2_psum, 1)
            nc.vector.tensor_scalar(scale[:, 2:3], sum2[:, 0:1], sum2[:, 1:2], 1.0 / WEIGHTS, ALU.add, ALU.mult).then_inc(s2_ready, 1)
            nc.vector.tensor_scalar(thr2[:, 0:1], sum2[:, 0:1], sum2[:, 1:2], 0.5 / WEIGHTS, ALU.add, ALU.mult).then_inc(s2_ready, 1)
            nc.vector.tensor_scalar(thr2[:, 1:2], sum2[:, 0:1], sum2[:, 1:2], -0.5 / WEIGHTS, ALU.add, ALU.mult).then_inc(s2_ready, 1)
            dve.wait_ge(s2_ready, 1)
            dve.wait_ge(thr_set, 3)
            nc.vector.tensor_tensor(s32[:, :], scale[:, 1:2], scale[:, 2:3], ALU.mult).then_inc(scale2_set, 1)

            def older_tap(s, i):
                k = TAPS - 1 - i
                for c in range(KC):
                    if i == 1:
                        dve.wait_ge(tap_set, KC * s + c + 1)
                    else:
                        dve.wait_ge(tap_step, KC * (TAPS - 2) * s + KC * (i - 2) + c + 1)
                    nc.vector.scalar_tensor_tensor(
                        out=conv[:, s, c], in0=xb[:, s, c, k:k + SEQ],
                        scalar=par[:, CONV_W + KC * k + c:CONV_W + KC * k + c + 1],
                        in1=conv[:, s, c], op0=ALU.mult, op1=ALU.add).then_inc(conv_set if i == TAPS - 1 else tap_step, 1)

            def first_mult(s):
                dve.wait_ge(conv_set, KC * (s + 1))
                nc.vector.memset(xb[:, s, :, TAPS - 1:TAPS], 0.5).then_inc(mult0_set, 1)

            def ternary_w2():
                dve.wait_ge(s2_ready, 3)
                dve.wait_ge(w13_q_set, 2)
                b2 = below[:, :, :].rearrange("p c n -> p (c n)")[:, 0:(FULL + 1) * D].rearrange("p (j d) -> p j d", d=D)
                nc.vector.tensor_scalar(b2, w2_raw[:, :, :], thr2[:, 1:2], None, ALU.is_lt).then_inc(below_set, 1)
                dve.wait_ge(below_set, 3)
                nc.vector.scalar_tensor_tensor(out=w2_q[:, :, :], in0=w2_raw[:, :, :], scalar=thr2[:, 0:1], in1=b2,
                                               op0=ALU.is_gt, op1=ALU.subtract).then_inc(w2_q_set, 1)

            def g_of(n):
                s, j = HJ[n]
                if n == 0:
                    dve.wait_ge(scale2_set, 1)
                dve.wait_ge(silu_set, n + 1)
                if n >= RING:
                    dve.wait_ge(g_lo_set, n - RING + 1)
                nc.vector.scalar_tensor_tensor(out=g[:, n % RING], in0=silu[:, n % RING], scalar=s32[:, 0:1],
                                               in1=slot[H_SLOT[s][j]][:, 1], op0=ALU.mult, op1=ALU.mult).then_inc(g_set, 1)

            def gated_input(s):
                dve.wait_ge(tx_set, KC * (s + 1))
                nc.vector.scalar_tensor_tensor(out=tx[:, s], in0=tx[:, s], scalar=1.0, in1=conv[:, s],
                                               op0=ALU.add, op1=ALU.mult).then_inc(nx_step, 1)

            def squares(s):
                dve.wait_ge(a_set, KC * (s + 1))
                nc.vector.tensor_tensor(xb[:, s, :, TAPS:], ta[:, s, :, 1:], ta[:, s, :, 1:], ALU.mult).then_inc(a2_set, 1)

            def recurrence(s):
                dve.wait_ge(mult0_set, s + 1)
                dve.wait_ge(nx_step, s + 1)
                dve.wait_ge(mult_set, KC * s + 1)
                nc.vector.tensor_tensor(tx[:, s, 0], tx[:, s, 0], xb[:, s, 0, TAPS - 1:], ALU.mult).then_inc(nx_set, 1)
                dve.wait_ge(y_set, KC * (s + 1))
                for c in range(KC):
                    dve.wait_ge((nx_set, nx_last_set)[c], s + 1)
                    nc.vector.tensor_tensor_scan(tx[:, s, c], ta[:, s, c], tx[:, s, c], 0.0, ALU.mult, ALU.add).then_inc(h_set, 1)
                    dve.wait_ge(h_set, KC * s + c + 1)
                    nc.vector.tensor_tensor(tx[:, s, c], tx[:, s, c], y[:, s, c], ALU.mult).then_inc(hy_set, 1)

            def lo_of_second_hy(c):
                dve.wait_ge(hy_lo_set, KC)
                dve.wait_ge(hy_hi_set, KC + c + 1)
                nc.vector.tensor_tensor(conv_lo[:, 1, c], tx[:, 1, c], conv_hi[:, 1, c].bitcast(f32), ALU.subtract).then_inc(hy_lo_set, 1)

            def output(n):
                s, i = O_ALL[n]
                dve.wait_ge(o_psum, n + 1)
                dve.wait_ge(x_res_set, TILES * (s + 1))
                t = slice(O_TILES[s][i].start, O_TILES[s][i].stop)
                nc.vector.tensor_tensor(x_sb[:, s, t], O_BANK[s][i][:, 0:len(O_TILES[s][i]) * D].rearrange("p (t d) -> p t d", d=D),
                                        x_sb[:, s, t], ALU.add).then_inc(o_set, 1)

            dve.wait_ge(sp_log, 1)
            nc.vector.scalar_tensor_tensor(out=sp_e[:, 1], in0=par[:, A_PARAM:A_PARAM + KC], scalar=0.0, in1=sp_e[:, 2],
                                           op0=ALU.max, op1=ALU.add).then_inc(rate_set, 1)
            dve.wait_ge(rate_set, 1)
            nc.vector.tensor_scalar(a_rate[:, :], sp_e[:, 1], -4.0, None, ALU.mult).then_inc(rate_set, 1)
            older_tap(0, 1)
            older_tap(0, 2)
            older_tap(0, 3)
            first_mult(0)
            g_of(0)
            g_of(1)
            older_tap(1, 1)
            g_of(2)
            older_tap(1, 2)
            g_of(3)
            older_tap(1, 3)
            first_mult(1)
            g_of(4)
            g_of(5)
            ternary_w2()
            g_of(6)
            gated_input(0)
            dve.wait_ge(silu_t_set, 1)
            nc.vector.scalar_tensor_tensor(out=g_t[HALF:HALF + TAIL], in0=silu_t[HALF:HALF + TAIL], scalar=s32[HALF:HALF + TAIL, 0:1],
                                           in1=slot[TAIL_SLOT][HALF:HALF + TAIL].rearrange("p s n -> p (s n)"), op0=ALU.mult, op1=ALU.mult).then_inc(g_t_set, 1)
            g_of(7)
            g_of(8)
            g_of(9)
            dve.wait_ge(g_hi_set, LAST_HI)
            for n in range(LAST_HI, 2 * FULL):
                dve.wait_ge(g_set, n + 1)
                nc.vector.tensor_copy(g_hi[:, HJ[n][1], HJ[n][0]], g[:, n % RING]).then_inc(g_hi_set, 1)
            dve.wait_ge(g_t_set, 1)
            dve.wait_ge(pads_set, 2)
            nc.vector.tensor_copy(gt_hi[HALF:HALF + TAIL].rearrange("p s n -> p (s n)"), g_t[HALF:HALF + TAIL]).then_inc(gt_hi_set, 1)
            squares(0)
            nc.vector.tensor_copy(gt[0:TAIL].rearrange("p s n -> p (s n)"), g_t[HALF:HALF + TAIL]).then_inc(gt_hi_set, 1)
            dve.wait_ge(gt_hi_set, 1)
            nc.vector.tensor_tensor(gt[HALF:HALF + TAIL].rearrange("p s n -> p (s n)"), g_t[HALF:HALF + TAIL],
                                    gt_hi[HALF:HALF + TAIL].rearrange("p s n -> p (s n)").bitcast(f32), ALU.subtract).then_inc(gt_lo_set, 1)
            gated_input(1)
            squares(1)
            recurrence(0)
            recurrence(1)
            lo_of_second_hy(0)
            output(0)
            lo_of_second_hy(1)
            for n in range(1, len(O_ALL)):
                output(n)

        @block.tensor
        def _(pe):
            def transposes(s):
                for t in range(TILES):
                    pe.wait_ge(xn_set, TILES * s + t + 1)
                    for c in range(KC):
                        mm = nc.tensor.transpose(xt_bank(s, 2 * t // TILES)[:, c, t * P % (SEQ // 2):t * P % (SEQ // 2) + P],
                                                 xn[:, s, t, c * P:(c + 1) * P], ident[:, :])
                    if 2 * (t + 1) % TILES == 0:
                        mm.then_inc(xt_psum, 1)

            def dense_terms(dst, m, terms, first, last, chunk_ready=None):
                for c in range(KC):
                    if chunk_ready:
                        pe.wait_ge(chunk_ready[0], chunk_ready[1] + c)
                    for o in range(KC):
                        for i, (w, v) in enumerate(terms):
                            mm = nc.tensor.matmul(dst[:, o], w[:, m, c, o * P:(o + 1) * P], v[:, c], start=(first and i == 0 and c == 0),
                                                  stop=(last and i == len(terms) - 1 and c == KC - 1))
                return mm

            def dense_product(dst, m, hi, lo, done, hi_ready=None, lo_ready=None, between=None):
                dense_terms(dst, m, [(w_hi, hi), (w_lo, hi)], True, False, hi_ready)
                if between:
                    between()
                dense_terms(dst, m, [(w_hi, lo)], False, True, lo_ready).then_inc(done, 1)

            def hidden(n):
                s, j = HJ[n]
                for o, col in enumerate((j * P, W3_AT + TAIL + j * P)):
                    for c in range(KC):
                        for v in (xt_hi, xt_lo):
                            mm = nc.tensor.matmul(slot[H_SLOT[s][j]][:, o], w13_q[:, c, col:col + P], v[:, s, c],
                                                  start=(c == 0 and v is xt_hi), stop=(c == KC - 1 and v is xt_lo))
                mm.then_inc(h_psum, 1)

            def hidden_tail():
                for s in range(SEQS):
                    for c in range(KC):
                        for v in (xt_hi, xt_lo):
                            mm = nc.tensor.matmul(slot[TAIL_SLOT][:, s], w13_q[:, c, FULL * P:(FULL + 1) * P], v[:, s, c],
                                                  start=(c == 0 and v is xt_hi), stop=(c == KC - 1 and v is xt_lo))
                mm.then_inc(t_psum, 1)

            def out_tile(s, i, t):
                at = (t - O_TILES[s][i].start) * D
                return O_BANK[s][i][:, at:at + D]

            def down(s):
                for j in range(FULL + 1):
                    if j < FULL:
                        pe.wait_ge(g_lo_set, FULL * s + j + 1)
                    else:
                        pe.wait_ge(gt_lo_set, 1)
                    for i, tiles in enumerate(O_TILES[s]):
                        for t in tiles:
                            rows = slice(t * P, (t + 1) * P)
                            parts = (g_hi[:, j], g_lo[:, j]) if j < FULL else (gt,)
                            for k, v in enumerate(parts):
                                nc.tensor.matmul(out_tile(s, i, t), v[:, s, rows], w2_q[:, j], start=(j == 0 and t == tiles.start and k == 0),
                                                 stop=False, skip_group_check=True)

            def project(s):
                pe.wait_ge(w_lo_set, WOUT + 1)

                def terms(i, ready, operands):
                    for c in range(KC):
                        pe.wait_ge(ready, KC * s + c + 1)
                        for t in O_TILES[s][i]:
                            for v, w in operands:
                                mm = nc.tensor.matmul(out_tile(s, i, t), v[:, s, c, t * P:(t + 1) * P], w[:, WOUT, c], start=False,
                                                      stop=(v is conv_lo and c == KC - 1), skip_group_check=True)
                    return mm

                def hi_terms(i):
                    terms(i, hy_hi_set, [(conv_hi, w_hi), (conv_hi, w_lo)])

                def lo_terms(i):
                    terms(i, hy_lo_set, [(conv_lo, w_hi)]).then_inc(o_psum, 1)

                banks = len(O_TILES[s])
                hi_terms(0)
                for i in range(1, banks):
                    hi_terms(i)
                    lo_terms(i - 1)
                lo_terms(banks - 1)

            pe.wait_ge(ones_set, 1)
            for _ in range(WARM):
                nc.tensor.matmul(slot[WARM_SLOT][:, 0, 0:P], ones[:, :], ones[:, :], start=True, stop=True)
            pe.wait_ge(ident_set, 1)
            transposes(0)

            def sum_of_w2():
                pe.wait_ge(abs2_set, 2)
                pe.wait_ge(xb_set, KC)
                nc.tensor.matmul(sum2, ones[:, :], abs_sum[:, 2:4], start=True, stop=True).then_inc(sum2_psum, 1)

            pe.wait_ge(w_lo_set, WX + 1)
            def first_x_terms(weights, part, ready):
                for h in range(2):
                    pe.wait_ge(ready, h + 1)
                    for c in range(KC):
                        for o in range(KC):
                            for w in weights:
                                mm = nc.tensor.matmul(slot[X_SLOT[0]][:, o, halves[h]], w[:, WX, c, o * P:(o + 1) * P],
                                                      part[:, 0, c, halves[h]],
                                                      start=(part is xt_hi and h == 0 and c == 0 and w is w_hi),
                                                      stop=(part is xt_lo and c == KC - 1), skip_group_check=True)
                return mm

            first_x_terms((w_hi, w_lo), xt_hi, xt_hi_set)
            pe.wait_ge(w_lo_set, WY + 1)
            dense_terms(slot[Y_SLOT[0]], WY, [(w_hi, xt_hi[:, 0]), (w_lo, xt_hi[:, 0])], True, False)
            transposes(1)
            pe.wait_ge(abs13_set, 2)
            pe.wait_ge(xt_lo_set, 1)
            nc.tensor.matmul(sums13, ones[:, :], abs_sum[:, 0:2], start=True, stop=True).then_inc(sum13_psum, 1)
            first_x_terms((w_hi,), xt_lo, xt_lo_set).then_inc(xb_psum, 1)
            dense_terms(slot[Y_SLOT[0]], WY, [(w_hi, xt_lo[:, 0])], False, True).then_inc(y_psum, 1)
            pe.wait_ge(thr_set, 3)
            pe.wait_ge(xt_hi_set, 4)
            dense_terms(slot[X_SLOT[1]], WX, [(w_hi, xt_hi[:, 1]), (w_lo, xt_hi[:, 1])], True, False)
            pe.wait_ge(xt_lo_set, 4)
            dense_terms(slot[X_SLOT[1]], WX, [(w_hi, xt_lo[:, 1])], False, True).then_inc(xb_psum, 1)
            dense_product(slot[Y_SLOT[1]], WY, xt_hi[:, 1], xt_lo[:, 1], y_psum, between=sum_of_w2)
            pe.wait_ge(w13_q_set, 2)
            pe.wait_ge(s2_ready, 3)
            hidden(0)
            pe.wait_ge(y_set, KC)
            hidden(1)
            pe.wait_ge(xb_set, 2 * KC)
            hidden(2)
            pe.wait_ge(y_set, 2 * KC)
            hidden(3)
            pe.wait_ge(g_set, 1)
            hidden(4)
            pe.wait_ge(g_set, 2)
            hidden(5)
            pe.wait_ge(g_set, 3)
            hidden(6)

            def gate_product(s, m, slots, done):
                pe.wait_ge(w_lo_set, m + 1)
                dense_product(slot[slots[s]], m, conv_hi[:, s], conv_lo[:, s], done,
                              (conv_hi_set, KC * s + 1), (conv_lo_set, KC * s + 1))

            pe.wait_ge(g_set, 4)
            gate_product(0, WIG, GX_SLOT, gx_psum)
            pe.wait_ge(g_set, 5)
            gate_product(0, WAG, GA_SLOT, ga_psum)
            pe.wait_ge(g_set, 6)
            hidden_tail()
            pe.wait_ge(g_set, 7)
            hidden(7)
            pe.wait_ge(tx_set, KC)
            hidden(8)
            pe.wait_ge(ta_set, KC)
            hidden(9)
            pe.wait_ge(g_t_set, 1)
            gate_product(1, WIG, GX_SLOT, gx_psum)
            pe.wait_ge(g_set, 8)
            gate_product(1, WAG, GA_SLOT, ga_psum)
            pe.wait_ge(w2_q_set, 1)
            pe.wait_ge(g_set, 9)
            down(0)
            pe.wait_ge(g_set, 10)
            pe.wait_ge(tx_set, 2 * KC)
            down(1)
            project(0)
            project(1)


def kernel(L0_attn_x, L0_attn_w_y, L0_attn_b_y, L0_attn_w_x, L0_attn_b_x, L0_attn_conv_w, L0_attn_conv_b,
           L0_attn_a_param, L0_attn_w_ig, L0_attn_b_ig, L0_attn_w_ag, L0_attn_b_ag, L0_attn_w_out, L0_attn_b_out,
           L0_ffn_w1, L0_ffn_w3, L0_ffn_w2):
    import numpy as np
    import concourse.bacc as bacc
    from concourse.bass_utils import run_bass_kernel_spmd

    x = np.ascontiguousarray(L0_attn_x)
    w3t = np.asarray(L0_ffn_w3).T
    vectors = [L0_attn_b_y, L0_attn_b_x, L0_attn_conv_b, L0_attn_a_param, L0_attn_b_ig, L0_attn_b_ag, *L0_attn_conv_w]
    arrays = {
        "x": x.reshape(TOKENS, D),
        "dense": np.stack([L0_attn_w_x, L0_attn_w_y, L0_attn_w_ig, L0_attn_w_ag, L0_attn_w_out]),
        "w13t": np.concatenate([np.asarray(L0_ffn_w1).T, w3t[:, FULL * P:], w3t[:, :FULL * P]], axis=1),
        "w2t": np.asarray(L0_ffn_w2).T,
        "params": np.stack(vectors).reshape(len(vectors) * KC, P).T,
        "b_out": np.asarray(L0_attn_b_out),
    }
    arrays = {k: np.ascontiguousarray(v) for k, v in arrays.items()}
    nc = bacc.Bacc("TRN2", target_bir_lowering=False, num_devices=1)
    aps = [nc.dram_tensor(k, v.shape, mybir.dt.from_np(v.dtype), kind="ExternalInput").ap() for k, v in arrays.items()]
    out = nc.dram_tensor("out", (TOKENS, D), mybir.dt.float32, kind="ExternalOutput").ap()
    build(nc, *aps, out)
    result = run_bass_kernel_spmd(nc, [arrays], core_ids=[0])
    return result.results[0]["out"].reshape(x.shape)
```
